# Optimizing a Trainium2 kernel written in Bass

```python
import numpy as np
import jax
import jax.numpy as jnp

def _softmax(x, axis=-1):
    return jax.nn.softmax(x, axis=axis)

def _gelu(x):
    return jax.nn.gelu(x, approximate=True)

def _silu(x):
    return jax.nn.silu(x)

def _sigmoid(x):
    return jax.nn.sigmoid(x)

def _layernorm(x, axis=-1, eps=1e-05):
    m = jnp.mean(x, axis=axis, keepdims=True)
    v = jnp.var(x, axis=axis, keepdims=True)
    return (x - m) / jnp.sqrt(v + eps)

def _scatter_add(tgt, idx, src, axis=0):
    return tgt.at[idx].add(src)

def _segment_sum(src, seg, n):
    return jax.ops.segment_sum(src, seg, n)
kernel_name = 'mk_flamingo_gated_d1_seqx_r2_3e1bbb'

def setup_inputs(seed: int=0):
    np.random.seed(seed)
    _w = jnp.asarray

    def _rec_inputs():
        import jax
        import jax.numpy as jnp
        _rk = jax.random.key(seed)
        x = 7.22e-05 + 1 * jax.random.normal(jax.random.fold_in(_rk, 1), (2, 2048, 512), jnp.float32)
        _lenS = 2048 - jax.random.randint(jax.random.fold_in(_rk, 7), (2,), 0, max(1, 2048 // 4) + 1, jnp.int32)
        _lenS2 = 128 - jax.random.randint(jax.random.fold_in(_rk, 8), (2,), 0, max(1, 128 // 4) + 1, jnp.int32)
        _ctx_1024P = jax.random.normal(jax.random.fold_in(_rk, 11), (2, 16, 512), jnp.float32)
        _ctx_1024c = jax.random.dirichlet(jax.random.fold_in(_rk, 511), 0.3 * jnp.ones((16,), jnp.float32), (2, 128))
        _ctx_1024t = jnp.einsum('bsk,bkd->bsd', _ctx_1024c, _ctx_1024P)
        _ctx_1024t = _ctx_1024t * jax.lax.rsqrt(jnp.mean(jnp.square(_ctx_1024t)) + 1e-12) * 0.953939
        ctx_1024 = 4.13588e-05 + 0.999923 * (_ctx_1024t + 0.3 * jax.random.normal(jax.random.fold_in(_rk, 611), (2, 128, 512), jnp.float32))
        _g = jax.random.normal(jax.random.fold_in(_rk, 9001), (2, 1), jnp.float32)
        _g = jnp.sign(_g) * jnp.maximum(jnp.abs(_g), 1.0) + (_g == 0) * 1.0
        g_xattn = _g[0]
        g_ffn = _g[1]
        return (x, ctx_1024, g_xattn, g_ffn)
    x, ctx_1024, g_xattn, g_ffn = _rec_inputs()

    def _L0_xattn_setup():
        import jax, jax.numpy as jnp
        import numpy as np
        N_HEAD = 16
        D_MODEL = 512
        D_K = D_MODEL // N_HEAD

        def _split_heads(x, B):
            return x.reshape(B, -1, N_HEAD, D_K).transpose(0, 2, 1, 3)
        key = jax.random.key(seed)
        ks = jax.random.split(key, 7)
        B, S = (4, 1024)
        scale = 1.0 / np.sqrt(D_MODEL)
        return {'Q': jax.random.normal(ks[0], (B, S, D_MODEL), jnp.float32), 'K': jax.random.normal(ks[1], (B, S, D_MODEL), jnp.float32), 'V': jax.random.normal(ks[2], (B, S, D_MODEL), jnp.float32), 'Wq': jax.random.normal(ks[3], (D_MODEL, D_MODEL), jnp.float32) * scale, 'bq': jnp.zeros((D_MODEL,), jnp.float32), 'Wo': jax.random.normal(ks[4], (D_MODEL, D_MODEL), jnp.float32) * scale, 'bo': jnp.zeros((D_MODEL,), jnp.float32)}
    _L0_xattn_all = _L0_xattn_setup()
    _L0_xattn_in = {k: v for k, v in _L0_xattn_all.items() if k in ('Wq', 'bq', 'Wo', 'bo')}
    del _L0_xattn_all

    def _L0_ffn_setup():
        import jax, jax.numpy as jnp
        import numpy as np
        EMBED = 512
        NUM_EXPERTS = 8
        TOP_K = 2
        key = jax.random.key(seed)
        ks = jax.random.split(key, 6)
        scale = EMBED ** (-0.5)
        return {'x': jax.random.normal(ks[0], (4, 2048, EMBED), jnp.float32), 'router_w': jax.random.normal(ks[1], (EMBED, NUM_EXPERTS), jnp.float32) * scale, 'router_b': jnp.zeros((NUM_EXPERTS,), jnp.float32), 'we_gate': jax.random.normal(ks[2], (NUM_EXPERTS, EMBED, EMBED), jnp.float32) * scale, 'we_up': jax.random.normal(ks[3], (NUM_EXPERTS, EMBED, EMBED), jnp.float32) * scale, 'we_down': jax.random.normal(ks[4], (NUM_EXPERTS, EMBED, EMBED), jnp.float32) * scale}
    _L0_ffn_all = _L0_ffn_setup()
    _L0_ffn_in = {k: v for k, v in _L0_ffn_all.items() if k in ('router_w', 'router_b', 'we_gate', 'we_up', 'we_down')}
    del _L0_ffn_all
    return {'x': x, 'ctx_1024': ctx_1024, 'g_xattn': g_xattn, 'g_ffn': g_ffn, 'L0_xattn_Wq': _L0_xattn_in['Wq'], 'L0_xattn_bq': _L0_xattn_in['bq'], 'L0_xattn_Wo': _L0_xattn_in['Wo'], 'L0_xattn_bo': _L0_xattn_in['bo'], 'L0_ffn_router_w': _L0_ffn_in['router_w'], 'L0_ffn_router_b': _L0_ffn_in['router_b'], 'L0_ffn_we_gate': _L0_ffn_in['we_gate'], 'L0_ffn_we_up': _L0_ffn_in['we_up'], 'L0_ffn_we_down': _L0_ffn_in['we_down']}

def reference(x, ctx_1024, g_xattn, g_ffn, L0_xattn_Wq, L0_xattn_bq, L0_xattn_Wo, L0_xattn_bo, L0_ffn_router_w, L0_ffn_router_b, L0_ffn_we_gate, L0_ffn_we_up, L0_ffn_we_down):
    import jax
    import jax.numpy as jnp

    def _L0_xattn_ref(Q, K, V, Wq, bq, Wo, bo):
        import jax, jax.numpy as jnp
        import numpy as np
        N_HEAD = 16
        D_MODEL = 512
        D_K = D_MODEL // N_HEAD

        def _split_heads(x, B):
            return x.reshape(B, -1, N_HEAD, D_K).transpose(0, 2, 1, 3)
        B = Q.shape[0]
        q = _split_heads(Q @ Wq + bq, B)
        k = _split_heads(K @ Wq + bq, B)
        v = _split_heads(V @ Wq + bq, B)
        scores = jnp.einsum('bhqd,bhkd->bhqk', q, k) / jnp.sqrt(jnp.asarray(D_K, q.dtype))
        attn = jax.nn.softmax(scores, axis=-1)
        out = jnp.einsum('bhqk,bhkd->bhqd', attn, v)
        out = out.transpose(0, 2, 1, 3).reshape(B, -1, D_MODEL)
        return out @ Wo + bo

    def _L0_ffn_ref(x, router_w, router_b, we_gate, we_up, we_down):
        import jax, jax.numpy as jnp
        import numpy as np
        EMBED = 512
        NUM_EXPERTS = 8
        TOP_K = 2
        x_shape = x.shape
        x_flat = x.reshape(-1, x_shape[-1])
        num_tokens = x_flat.shape[0]
        router_logits = x_flat @ router_w + router_b
        topk_weights, topk_indices = jax.lax.top_k(router_logits, k=TOP_K)
        topk_weights = jax.nn.softmax(topk_weights, axis=-1)
        token_idx_mesh = jnp.repeat(jnp.arange(num_tokens), TOP_K)
        expert_idx_mesh = topk_indices.reshape(-1)
        sort_permutation = jnp.argsort(expert_idx_mesh)
        sorted_expert_idx = expert_idx_mesh[sort_permutation]
        sorted_token_idx = token_idx_mesh[sort_permutation]
        group_sizes = jnp.bincount(sorted_expert_idx, length=NUM_EXPERTS)
        sorted_tokens = x_flat[sorted_token_idx]
        ff_gate = jax.lax.ragged_dot(sorted_tokens, we_gate, group_sizes)
        ff_up = jax.lax.ragged_dot(sorted_tokens, we_up, group_sizes)
        activated = jax.nn.silu(ff_gate) * ff_up
        ff_out = jax.lax.ragged_dot(activated, we_down, group_sizes)
        sorted_weights = topk_weights.reshape(-1)[sort_permutation]
        ff_out = ff_out * sorted_weights[:, None]
        output_flat = jnp.zeros_like(x_flat).at[sorted_token_idx].add(ff_out)
        return output_flat.reshape(x_shape)
    x = x + jnp.tanh(g_xattn[0]) * _L0_xattn_ref(_layernorm(x, axis=-1), ctx_1024, ctx_1024, L0_xattn_Wq, L0_xattn_bq, L0_xattn_Wo, L0_xattn_bo)
    x = x + jnp.tanh(g_ffn[0]) * _L0_ffn_ref(_layernorm(x, axis=-1), L0_ffn_router_w, L0_ffn_router_b, L0_ffn_we_gate, L0_ffn_we_up, L0_ffn_we_down)
    return x

_drawn_inputs = setup_inputs


def setup_inputs(seed=0):
    import zlib

    import numpy as np

    out = dict(_drawn_inputs(seed))
    spreads = {'L0_xattn_bq': (0.0, 0.1), 'L0_xattn_bo': (0.0, 0.1), 'L0_ffn_router_b': (0.0, 0.1)}
    factors = {}
    for name, (base, spread) in spreads.items():
        noise = np.random.default_rng([zlib.crc32(name.encode()), seed]).standard_normal(out[name].shape)
        drawn = base * np.exp(spread * noise) if base else spread * noise
        out[name] = jnp.asarray(drawn.astype(out[name].dtype))
    for name, factor in factors.items():
        out[name] = (out[name] * factor).astype(out[name].dtype)
    return out
```

```python
import numpy as np
import concourse.bass as bass
from concourse import mybir
from contextlib import ExitStack

F32 = mybir.dt.float32
F32R = mybir.dt.float32r
F16 = mybir.dt.float16
BF16 = mybir.dt.bfloat16
I32 = mybir.dt.int32
U32 = mybir.dt.uint32
ALU = mybir.AluOpType
ACT = mybir.ActivationFunctionType
AX_X = mybir.AxisListType.X

P = 128
BATCHES, SEQ, D = 2, 2048, 512
TOKENS = BATCHES * SEQ
DC = D // P
HEADS, DK, KEYS = 16, 32, 128
PER_CHUNK = P // DK
BLOCK = 512
SUB = BLOCK // P
BLOCKS = TOKENS // BLOCK
LAST = BLOCKS - 1
EXPERTS, TOPK = 8, 2
EPS = 1e-5
LAG = 3
ROW = D + 8
W_DIFF, W_LOW, FIRST_EXPERT, TOKEN = D, D + 1, D + 2, D + 3
REGION = TOKENS + P
DUMMY = EXPERTS * REGION
SORTED_ROWS = DUMMY + P
SLOTS = TOKENS * TOPK // P + EXPERTS - 1
SLOTS_PAD = SLOTS + 1
RING = 4
MATS = 3
PROB_SCALE = 4096.0
X_SCALE = 2048.0


def wait(eng, sem, value):
    if isinstance(value, int) and value <= 0:
        return
    eng.wait_ge(sem, value)


def hold(eng, spare, held, n):
    wait(eng, held, n)
    eng.tensor_tensor(spare[0:1, 0:1], spare[0:1, 1:2], spare[0:1, 1:2], ALU.add).then_inc(held, 1)


class Blk:

    def __init__(self, q, b):
        self.q, self.b, self.n = q, b, q * BATCHES + b
        self.first = isinstance(self.n, int) and self.n == 0
        self.last = isinstance(self.n, int) and self.n == LAST

    def f_transposes(self, u):
        return self.n * 32 + (u if self.first else u - 8)

    def f_queries(self, u):
        return self.f_transposes(u + 4)

    def f_maxima(self, u):
        return self.f_transposes(u + 8)

    def f_output(self, u):
        return self.n * 32 + (48 - (24 if self.last else 0) + u)

    def f_routing(self, u):
        return self.n * 32 + (52 - (24 if self.last else 0) + u)


def attention_and_routing(nc, A, out, rows_sorted, counts_dram):
    with ExitStack() as ctx:
        def sb(name, shape, dt):
            return ctx.enter_context(nc.sbuf_tensor(name, shape, dt))

        def bank(name, dt=F32, n=512):
            return ctx.enter_context(nc.psum_tensor(name, [P, n], dt))

        def sem(name):
            return ctx.enter_context(nc.semaphore(name))

        wq_hi, wq_lo = sb("wq_hi", [P, DC, D], F32R), sb("wq_lo", [P, DC, D], F32R)
        wo_hi, wo_lo = sb("wo_hi", [P, DC, D], F32R), sb("wo_lo", [P, DC, D], F32R)
        k_hi = [sb(f"k_hi{b}", [P, DC, PER_CHUNK, KEYS], F32R) for b in range(BATCHES)]
        k_lo = [sb(f"k_lo{b}", [P, DC, PER_CHUNK, KEYS], F32R) for b in range(BATCHES)]
        v_parts = [sb(f"v_parts{b}", [P, 3, D], BF16) for b in range(BATCHES)]
        ident = sb("ident", [P, P], F32)
        ident_bf = sb("ident_bf", [P, P], BF16)
        ones_bf = sb("ones_bf", [P, P], BF16)
        before = sb("before", [P, P], BF16)
        minus_head = sb("minus_head", [P, HEADS, KEYS], BF16)
        bq_col = sb("bq_col", [P, DC], F32)
        bq_row = sb("bq_row", [P, D], F32)
        bo_row = sb("bo_row", [P, D], F32)
        rb_row = sb("rb_row", [P, EXPERTS], F32)
        wr = sb("wr", [P, DC, EXPERTS], F32)
        wr_rest = sb("wr_rest", [P, 2, DC, EXPERTS], F32)
        wr_parts = sb("wr_parts", [P, DC, 3, EXPERTS], BF16)
        gates = sb("gates", [P, 2], F32)
        tanh_g = sb("tanh_g", [P, 2], F32)
        minus_half = sb("minus_half", [P, SUB], F32)
        eps = sb("eps", [P, SUB], F32)
        spare_pool, spare_dve = sb("spare_pool", [1, 2], F32), sb("spare_dve", [1, 2], F32)
        exp_bias = sb("exp_bias", [P, 1], F32)
        iota_i = sb("iota_i", [P, SUB, EXPERTS], I32)
        iota_f = sb("iota_f", [P, SUB, EXPERTS], F32)
        region_f = sb("region_f", [P, SUB, EXPERTS], F32)
        tok_i = [sb(f"tok_i{b}", [P, SUB], I32) for b in range(BATCHES)]
        tok_f = [sb(f"tok_f{b}", [P, SUB], F32) for b in range(BATCHES)]
        x = [sb(f"x{b}", [P, SUB, D], F32) for b in range(BATCHES)]
        xn = sb("xn", [P, SUB, D], F32)
        xt_hi, xt_lo = sb("xt_hi", [P, DC, BLOCK], F32R), sb("xt_lo", [P, DC, BLOCK], F32R)
        q_hi, q_lo = sb("q_hi", [P, DC, BLOCK], F32R), sb("q_lo", [P, DC, BLOCK], F32R)
        o_hi, o_lo = sb("o_hi", [P, DC, BLOCK], F32R), sb("o_lo", [P, DC, BLOCK], F32R)
        stats1, mv1 = sb("stats1", [P, SUB, 6], F32), sb("mv1", [P, SUB, 2], F32)
        stats2, mv2 = sb("stats2", [P, SUB, 6], F32), sb("mv2", [P, SUB, 2], F32)
        var1, rstd1 = sb("var1", [P, SUB], F32), sb("rstd1", [P, SUB], F32)
        var2, rstd2 = sb("var2", [P, SUB], F32), sb("rstd2", [P, SUB], F32)
        mx = sb("mx", [P, SUB, HEADS], F32)
        mx_rest = sb("mx_rest", [P, SUB, HEADS], F32)
        mx_parts = sb("mx_parts", [P, SUB, 2 * HEADS], BF16)
        mx_t = sb("mx_t", [P, BLOCK], BF16)
        prob = sb("prob", [P, 4, BLOCK], F32)
        p_hi, p_lo = sb("p_hi", [P, 4, BLOCK], F16), sb("p_lo", [P, 4, BLOCK], F16)
        rden = sb("rden", [P, BLOCK], F32)
        o_f = sb("o_f", [P, 2, BLOCK], F32)
        rows = sb("rows", [P, SUB, ROW], F32)
        r_hi, r_lo = sb("r_hi", [P, SUB, D], F16), sb("r_lo", [P, SUB, D], F16)
        lsum = sb("lsum", [P, SUB, EXPERTS], F32)
        logits = sb("logits", [P, SUB, EXPERTS], F32)
        top = sb("top", [P, SUB, 8], F32)
        top_ix = sb("top_ix", [P, SUB, 8], U32)
        pick = sb("pick", [P, SUB, TOPK], F32)
        chosen = [sb(f"chosen{k}", [P, SUB, EXPERTS], F32) for k in range(TOPK)]
        chosen_any = sb("chosen_any", [P, SUB, EXPERTS], BF16)
        earlier = sb("earlier", [P, SUB + 1, EXPERTS], BF16)
        wdiff, wexp, wden, wrec = (sb(n, [P, SUB], F32) for n in ("wdiff", "wexp", "wden", "wrec"))
        whigh = sb("whigh", [P, SUB], F32)
        place = sb("place", [P, SUB, EXPERTS], F32)
        place_k = sb("place_k", [P, TOPK, SUB, EXPERTS], F32)
        place_s = sb("place_s", [P, TOPK, SUB], F32)
        target = sb("target", [P, TOPK, SUB], I32)
        counts = sb("counts", [P, EXPERTS], F32)

        psF = [bank(f"psF{i}") for i in range(2)]
        psB = [bank(f"psB{i}") for i in range(2)]
        psO, psD = bank("psO"), bank("psD")
        psM = bank("psM", BF16, 1024)
        psL = bank("psL")
        LG = psL[:, 0:SUB * 32].rearrange("p (s w) -> p s w", w=32)
        RK = psL[:, 256:256 + SUB * EXPERTS].rearrange("p (s e) -> p s e", e=EXPERTS)
        TOTAL = psL[:, 384:384 + EXPERTS]

        small_in, wq_in, wo_in, ctx_in = sem("small_in"), sem("wq_in"), sem("wo_in"), sem("ctx_in")
        const_set, const_cut, const_f = sem("const_set"), sem("const_cut"), sem("const_f")
        tanh_done, gated = sem("tanh_done"), sem("gated")
        w_hi_done, w_lo_done = sem("w_hi_done"), sem("w_lo_done")
        wr_done = sem("wr_done")
        ctx_t, ctx_hi, ctx_lo = sem("ctx_t"), sem("ctx_hi"), sem("ctx_lo")
        kv_full, kv_done, v_done = sem("kv_full"), sem("kv_done"), sem("v_done")
        kt_full, kt_hi, kt_lo = sem("kt_full"), sem("kt_hi"), sem("kt_lo")
        held_dve, held_pool = sem("held_dve"), sem("held_pool")
        x_in = [sem(f"x_in{b}") for b in range(BATCHES)]
        x2_out = [sem(f"x2_out{b}") for b in range(BATCHES)]
        stats1_done, mv1_done, var1_done, rstd1_done = (sem(n) for n in ("stats1_done", "mv1_done", "var1_done", "rstd1_done"))
        stats2_done, mv2_done, var2_done, rstd2_done = (sem(n) for n in ("stats2_done", "mv2_done", "var2_done", "rstd2_done"))
        xn_done, xb_done, xn2_done = sem("xn_done"), sem("xb_done"), sem("xn2_done")
        f_full, f_free = sem("f_full"), sem("f_free")
        xt_hi_done, q_hi_done, r_hi_done = sem("xt_hi_done"), sem("q_hi_done"), sem("r_hi_done")
        mx_step, mx_full, mx_t_done = sem("mx_step"), sem("mx_full"), sem("mx_t_done")
        b_full, exp_done, p_lo_done, pv_done = (sem(n) for n in ("b_full", "exp_done", "p_lo_done", "pv_done"))
        rden_done, o_done, o_hi_done, o_lo_done = (sem(n) for n in ("rden_done", "o_done", "o_hi_done", "o_lo_done"))
        lg_full, route_step, wexp_done, meta_done = sem("lg_full"), sem("route_step"), sem("wexp_done"), sem("meta_done")
        rk_full, place_step, scattered = sem("rk_full"), sem("place_step"), sem("scattered")
        total_full, counts_done, counts_out = sem("total_full"), sem("counts_done"), sem("counts_out")

        wq_raw, wo_raw, ctx_raw, kv = xn, x[1], o_f, rden
        SMALL = 7
        CONST_SET, CONST_CUT = 22, 5
        ROUTE = 4 + 4 + 4 + 1 + 4 + 4
        x_rows = [A["x"][b].rearrange("(q s p) d -> q p s d", p=P, s=SUB) for b in range(BATCHES)]
        out_rows = [out[b * SEQ:(b + 1) * SEQ, :].rearrange("(q s p) d -> q p s d", p=P, s=SUB) for b in range(BATCHES)]

        block = ctx.enter_context(nc.Block())

        @block.sync
        def _(sp):
            for k, dst, src in (
                ("small", bq_col[:, :], A["bq"].rearrange("(c p) -> p c", p=P)),
                ("small", bq_row[:, :], A["bq"].partition_broadcast(P)),
                ("small", bo_row[:, :], A["bo"].partition_broadcast(P)),
                ("small", rb_row[:, :], A["router_b"].partition_broadcast(P)),
                ("small", wr[:, :, :], A["router_w"].rearrange("(c p) e -> p c e", p=P)),
                ("small", gates[:, 0:1], A["g_xattn"].partition_broadcast(P)),
                ("small", gates[:, 1:2], A["g_ffn"].partition_broadcast(P)),
            ):
                with nc.allow_non_contiguous_dma(reason="a bias by partition"):
                    sp.dma_start(dst, src).then_inc(small_in, 16)
            sp.dma_start(ctx_raw[:, :, :], A["ctx"].rearrange("b p d -> p b d")).then_inc(ctx_in, 16)
            sp.dma_start(wq_raw[:, :, :], A["Wq"].rearrange("(c p) n -> p c n", p=P)).then_inc(wq_in, 16)
            sp.dma_start(wo_raw[:, :, :], A["Wo"].rearrange("(c p) n -> p c n", p=P)).then_inc(wo_in, 16)

            def load_x(nxt):
                if isinstance(nxt.n, int) and nxt.n == 1:
                    sp.wait_ge(w_lo_done, 2)
                elif not nxt.first:
                    sp.wait_ge(x2_out[nxt.b], 16 * nxt.q)
                    sp.wait_ge(xn2_done, nxt.n - 1)
                sp.dma_start(x[nxt.b][:, :, :], x_rows[nxt.b][at(nxt.q)].squeeze(0)).then_inc(x_in[nxt.b], 16)

            def store_x2(cur):
                sp.wait_ge(f_free, cur.f_output(3) + 1)
                sp.dma_start(out_rows[cur.b][at(cur.q)].squeeze(0), x[cur.b][:, :, :]).then_inc(x2_out[cur.b], 16)

            def step(cur, nxt):
                if nxt:
                    load_x(nxt)
                store_x2(cur)

            load_x(Blk(0, 0))
            step(Blk(0, 0), Blk(0, 1))
            with sp.Fori(0, BLOCKS // 2 - 1, 1) as j:
                step(Blk(j, 1), Blk(j + 1, 0))
                step(Blk(j + 1, 0), Blk(j + 1, 1))
            step(Blk(BLOCKS // 2 - 1, 1), None)
            for b in range(BATCHES):
                sp.wait_ge(x2_out[b], 16 * BLOCKS // 2)

        @block.gpsimd
        def _(pool):
            for t, v in ((ident, 0.0), (ident_bf, 0.0), (ones_bf, 1.0), (before, 1.0), (minus_head, 0.0),
                         (minus_half, -0.5), (eps, EPS), (spare_pool, 0.0), (spare_dve, 0.0), (exp_bias, float(np.log(PROB_SCALE))), (mx_t, 0.0), (earlier, 0.0), (rows, 0.0),
                         *((k, 0.0) for k in k_hi + k_lo)):
                pool.memset(t[:].bitcast(F32) if t in k_hi + k_lo else t[:], v).then_inc(const_set, 1)
            pool.iota(iota_i[:, :, :], pattern=[[0, SUB], [1, EXPERTS]], base=0, channel_multiplier=0).then_inc(const_set, 1)
            for b in range(BATCHES):
                pool.iota(tok_i[b][:, :], pattern=[[P, SUB]], base=b * SEQ, channel_multiplier=1).then_inc(const_set, 1)
            pool.memset(counts[:, :], 0.0).then_inc(const_set, 1)
            pool.memset(mx[:], 0.0).then_inc(const_set, 1)
            pool.wait_ge(const_set, CONST_SET)
            for t in (ident, ident_bf):
                pool.affine_select(out=t[:, :], in_=t[:, :], compare_op=ALU.not_equal, fill=1.0, base=0,
                                   pattern=[[-1, P]], channel_multiplier=1).then_inc(const_cut, 1)
            pool.affine_select(out=before[:, :], in_=before[:, :], compare_op=ALU.is_gt, fill=0.0, base=0,
                               pattern=[[1, P]], channel_multiplier=-1).then_inc(const_cut, 1)
            for part in range(2):
                if part:
                    pool.wait_ge(const_cut, 4)
                pool.affine_select(out=minus_head[:, :, :], in_=minus_head[:, :, :], compare_op=ALU.not_equal, fill=-1.0,
                                   base=-part * HEADS, pattern=[[-1, HEADS], [0, KEYS]],
                                   channel_multiplier=1).then_inc(const_cut, 1)

            def rstd(n, mv, var, rs, mv_done, var_done, rstd_done):
                pool.wait_ge(mv_done, n * SUB + SUB)
                pool.tensor_tensor(var[:, :], mv[:, :, 1], eps[:, :], ALU.add).then_inc(var_done, 1)
                pool.wait_ge(var_done, n + 1)
                pool.tensor_tensor(rs[:, :], var[:, :], minus_half[:, :], ALU.pow).then_inc(rstd_done, 1)

            def rstd_first(nxt):
                rstd(nxt.n, mv1, var1, rstd1, mv1_done, var1_done, rstd1_done)

            def rstd_second(cur):
                rstd(cur.n, mv2, var2, rstd2, mv2_done, var2_done, rstd2_done)

            def out_lo(cur, c):
                pool.wait_ge(o_hi_done, cur.n * DC + c + 1)
                pool.tensor_tensor(o_lo[:, c, :], o_f[:, c % 2, :], o_hi[:, c, :].bitcast(F32), ALU.subtract).then_inc(o_lo_done, 1)

            def add_bias(nxt):
                pool.wait_ge(xn_done, nxt.n + 1)
                if nxt.first:
                    pool.wait_ge(gated, 2)
                for s in range(SUB):
                    last = pool.tensor_tensor(x[nxt.b][:, s, :], x[nxt.b][:, s, :], bo_row[:, :], ALU.add)
                last.then_inc(xb_done, 1)

            def scatter(prv):
                pool.wait_ge(place_step, prv.n * 5 + 5)
                pool.wait_ge(meta_done, prv.n * 6 + 6)
                hold(pool, spare_pool, held_pool, prv.n)
                for k in range(TOPK):
                    for s in range(SUB):
                        pool.indirect_dma_start(
                            out=rows_sorted, out_offset=bass.IndirectOffsetOnAxis(ap=target[:, k, s:s + 1].bitcast(U32), axis=0),
                            in_=rows[:, s, :], in_offset=None, bounds_check=SORTED_ROWS - 1, oob_is_err=True).then_inc(scattered, 16)

            def step(cur, nxt, prv):
                if nxt:
                    rstd_first(nxt)
                out_lo(cur, 0)
                if nxt:
                    add_bias(nxt)
                out_lo(cur, 1)
                out_lo(cur, 2)
                if prv:
                    scatter(prv)
                out_lo(cur, 3)
                rstd_second(cur)

            rstd_first(Blk(0, 0))
            add_bias(Blk(0, 0))
            step(Blk(0, 0), Blk(0, 1), None)
            with pool.Fori(0, BLOCKS // 2 - 1, 1) as j:
                step(Blk(j, 1), Blk(j + 1, 0), Blk(j, 0))
                step(Blk(j + 1, 0), Blk(j + 1, 1), Blk(j, 1))
            step(Blk(BLOCKS // 2 - 1, 1), None, Blk(BLOCKS // 2 - 1, 0))
            scatter(Blk(BLOCKS // 2 - 1, 1))
            pool.wait_ge(scattered, 16 * TOPK * SUB * BLOCKS)
            pool.wait_ge(counts_done, 1)
            pool.dma_start(counts_dram, counts[:, :]).then_inc(counts_out, 16)
            pool.wait_ge(counts_out, 16)

        @block.scalar
        def _(act):
            act.wait_ge(small_in, 16 * SMALL)
            act.activation(tanh_g[:, :], gates[:, :], ACT.Tanh).then_inc(tanh_done, 1)
            act.wait_ge(wq_in, 16)
            act.activation(wq_hi[:, :, :], wq_raw[:, :, :], ACT.Copy).then_inc(w_hi_done, 1)
            act.wait_ge(gated, 2)
            act.activation(wo_hi[:, :, :], wo_raw[:, :, :], ACT.Copy).then_inc(w_hi_done, 1)
            for b in range(BATCHES):
                act.wait_ge(ctx_t, b + 1)
                wait(act, kv_full, b)
                act.activation(o_hi[:, 0, :], psF[0][:, :], ACT.Copy).then_inc(ctx_hi, 1)
                act.wait_ge(kt_full, b + 1)
                if b == 0:
                    act.wait_ge(const_set, CONST_SET)
                for i in range(PER_CHUNK):
                    r = slice(DK * i, DK * i + DK)
                    last = act.activation(k_hi[b][r, :, i, :], psF[1][r, :].rearrange("p (c k) -> p c k", c=DC), ACT.Copy)
                last.then_inc(kt_hi, 1)

            def halves(nxt):
                for c in range(DC):
                    act.wait_ge(f_full, nxt.f_transposes(c) + 1)
                    act.activation(xt_hi[:, c, :], psF[c % 2][:, :], ACT.Copy).then_inc(xt_hi_done, 1)

            def queries(nxt):
                for m in range(DC):
                    act.wait_ge(f_full, nxt.f_queries(m) + 1)
                    act.activation(q_hi[:, m, :], psF[m % 2][:, :], ACT.Identity, bias=bq_col[:, m:m + 1]).then_inc(q_hi_done, 1)

            def exps(cur, hs):
                for h in hs:
                    c = cur.n * HEADS + h
                    act.wait_ge(b_full, c + 1)
                    wait(act, pv_done, c - 3)
                    act.activation(p_hi[:, h % 4, :], psB[h % 2][:, :], ACT.Exp, bias=exp_bias[:, 0:1],
                                   scale=float(DK) ** -0.5)
                    act.activation(prob[:, h % 4, :], psB[h % 2][:, :], ACT.Exp, bias=exp_bias[:, 0:1],
                                   scale=float(DK) ** -0.5).then_inc(exp_done, 1)

            def out_hi(cur, c):
                act.wait_ge(o_done, cur.n * DC + c + 1)
                if c == 0 and not cur.first:
                    act.wait_ge(f_full, cur.n * 32 + 20)
                act.activation(o_hi[:, c, :], o_f[:, c % 2, :], ACT.Copy).then_inc(o_hi_done, 1)

            def routing_hi(prv):
                for s in range(SUB):
                    act.wait_ge(f_full, prv.f_routing(s) + 1)
                    act.activation(r_hi[:, s, :], psF[s % 2][:, :], ACT.Copy, scale=X_SCALE).then_inc(r_hi_done, 1)

            def weight_exp(prv):
                act.wait_ge(route_step, prv.n * ROUTE + ROUTE)
                act.activation(wexp[:, :], wdiff[:, :], ACT.Exp).then_inc(wexp_done, 1)

            def step(cur, nxt, prv):
                exps(cur, range(0, 4))
                if prv:
                    routing_hi(prv)
                exps(cur, range(4, 8))
                out_hi(cur, 0)
                exps(cur, range(8, 12))
                out_hi(cur, 1)
                if prv:
                    weight_exp(prv)
                if nxt:
                    halves(nxt)
                exps(cur, range(12, 16))
                out_hi(cur, 2)
                if nxt:
                    queries(nxt)
                out_hi(cur, 3)

            halves(Blk(0, 0))
            queries(Blk(0, 0))
            step(Blk(0, 0), Blk(0, 1), None)
            with act.Fori(0, BLOCKS // 2 - 1, 1) as j:
                step(Blk(j, 1), Blk(j + 1, 0), Blk(j, 0))
                step(Blk(j + 1, 0), Blk(j + 1, 1), Blk(j, 1))
            step(Blk(BLOCKS // 2 - 1, 1), None, Blk(BLOCKS // 2 - 1, 0))
            routing_hi(Blk(BLOCKS // 2 - 1, 1))
            weight_exp(Blk(BLOCKS // 2 - 1, 1))

        @block.tensor
        def _(pe):
            def split3(dst, hi, lo, w_hi, w_lo, m, start=True, stop=True):
                for c in range(DC):
                    pe.matmul(dst, hi(c), w_hi[:, c, m], start=start and c == 0, stop=False)
                    pe.matmul(dst, hi(c), w_lo[:, c, m], start=False, stop=False)
                    last = pe.matmul(dst, lo(c), w_hi[:, c, m], start=False, stop=stop and c == DC - 1)
                return last

            pe.wait_ge(const_cut, CONST_CUT)
            pe.wait_ge(ctx_in, 16)
            for b in range(BATCHES):
                wait(pe, ctx_lo, b)
                for c in range(DC):
                    last = pe.transpose(psF[0][:, c * P:c * P + P], ctx_raw[:, b, c * P:c * P + P], ident[:, :])
                last.then_inc(ctx_t, 1)
                pe.wait_ge(ctx_lo, b + 1)
                pe.wait_ge(w_lo_done, 1)
                wait(pe, kv_done, b)
                split3(psB[0][:, :], lambda c: o_hi[:, 0, c * P:c * P + P], lambda c: o_lo[:, 0, c * P:c * P + P],
                       wq_hi, wq_lo, slice(0, D)).then_inc(kv_full, 1)
                pe.wait_ge(kv_done, b + 1)
                wait(pe, kt_lo, b)
                for c in range(DC):
                    last = pe.transpose(psF[1][:, c * P:c * P + P], kv[:, c * P:c * P + P], ident[:, :])
                last.then_inc(kt_full, 1)
            pe.wait_ge(kt_lo, BATCHES)
            pe.wait_ge(v_done, BATCHES * 5)
            pe.wait_ge(w_lo_done, 2)
            pe.wait_ge(wr_done, 5)

            def transposes(nxt):
                pe.wait_ge(xn_done, nxt.n + 1)
                for c in range(DC):
                    wait(pe, f_free, nxt.f_transposes(c) - 1)
                    for s in range(SUB):
                        last = pe.transpose(psF[c % 2][:, s * P:s * P + P], xn[:, s, c * P:c * P + P], ident[:, :])
                    last.then_inc(f_full, 1)

            def queries(nxt):
                pe.wait_ge(f_free, nxt.f_transposes(3) + 1)
                for m in range(DC):
                    pe.wait_ge(f_free, nxt.f_queries(m) - 1)
                    for c in range(DC):
                        ms = slice(m * P, m * P + P)
                        pe.matmul(psF[m % 2][:, :], wq_hi[:, c, ms], xt_hi[:, c, :], start=c == 0, stop=False)
                        pe.matmul(psF[m % 2][:, :], wq_hi[:, c, ms], xt_lo[:, c, :], start=False, stop=False)
                        last = pe.matmul(psF[m % 2][:, :], wq_lo[:, c, ms], xt_hi[:, c, :], start=False, stop=c == DC - 1)
                    last.then_inc(f_full, 1)

            def maxima(nxt):
                pe.wait_ge(f_free, nxt.f_queries(3) + 1)
                for s in range(SUB):
                    for c in range(DC):
                        u = s * DC + c
                        pe.wait_ge(f_free, nxt.f_maxima(u) - 1)
                        pe.matmul(psF[u % 2][:, :], q_hi[:, c, s * P:s * P + P],
                                  k_hi[nxt.b][:, c, :, :].rearrange("p i k -> p (i k)"), start=True, stop=True).then_inc(f_full, 1)

            def maxima_t(nxt):
                pe.wait_ge(mx_step, nxt.n * 3 + 3)
                for s in range(SUB):
                    last = pe.transpose(psM[0:2 * HEADS, s * P:s * P + P], mx_parts[:, s, :], ident_bf[:, :])
                last.then_inc(mx_full, 1)

            def scores(cur, h):
                n, c, i = cur.n * HEADS + h, h // PER_CHUNK, h % PER_CHUNK
                if h == 0:
                    pe.wait_ge(mx_t_done, cur.n + 1)
                wait(pe, exp_done, n - 1)
                dst = psB[h % 2][:, :]
                pe.matmul(dst, k_hi[cur.b][:, c, i, :], q_hi[:, c, :], start=True, stop=False)
                pe.matmul(dst, k_hi[cur.b][:, c, i, :], q_lo[:, c, :], start=False, stop=False)
                pe.matmul(dst, k_lo[cur.b][:, c, i, :], q_hi[:, c, :], start=False, stop=False)
                pe.matmul(dst, minus_head[:, h, :], mx_t[:, :], start=False, stop=True).then_inc(b_full, 1)

            def values(cur, h):
                n, c, i = cur.n * HEADS + h, h // PER_CHUNK, h % PER_CHUNK
                pe.wait_ge(p_lo_done, n + 1)
                if i == 0:
                    wait(pe, o_done, cur.n * DC + c)
                r = slice(DK * i, DK * i + DK)
                hi, lo = p_hi[:, h % 4, :], p_lo[:, h % 4, :]
                v = [v_parts[cur.b][:, k, h * DK:h * DK + DK] for k in range(3)]
                for k, (part, p) in enumerate(((v[0], hi), (v[1], hi), (v[2], hi), (v[0], lo), (v[1], lo))):
                    pe.matmul(psO[r, :], part, p, start=k == 0, stop=k == 4)
                pe.matmul(psD[r, :], ones_bf[:, 0:DK], hi, start=True, stop=False)
                pe.matmul(psD[r, :], ones_bf[:, 0:DK], lo, start=False, stop=True).then_inc(pv_done, 1)

            def heads(cur, hs):
                for h in hs:
                    scores(cur, h)
                    if h >= LAG:
                        values(cur, h - LAG)

            def output(cur):
                pe.wait_ge(o_lo_done, cur.n * DC + DC)
                for s in range(SUB):
                    pe.wait_ge(f_free, cur.f_output(s) - 1)
                    ss = slice(s * P, s * P + P)
                    split3(psF[s % 2][:, :], lambda c: o_hi[:, c, ss], lambda c: o_lo[:, c, ss],
                           wo_hi, wo_lo, slice(0, D)).then_inc(f_full, 1)

            def routing_t(prv):
                pe.wait_ge(xn2_done, prv.n + 1)
                for s in range(SUB):
                    pe.wait_ge(f_free, prv.f_routing(s) - 1)
                    for c in range(DC):
                        last = pe.transpose(psF[s % 2][:, c * P:c * P + P], rows[:, s, c * P:c * P + P], ident[:, :])
                    last.then_inc(f_full, 1)

            def routing_logits(prv):
                pe.wait_ge(f_free, prv.f_routing(3) + 1)
                wait(pe, place_step, prv.n * 5)
                for s in range(SUB):
                    for c in range(DC):
                        for k, half in enumerate((r_hi, r_lo)):
                            last = pe.matmul(LG[:, s, 0:3 * EXPERTS], half[:, s, c * P:c * P + P],
                                             wr_parts[:, c, :, :].rearrange("p k e -> p (k e)"),
                                             start=c == 0 and k == 0, stop=c == DC - 1 and k == 1)
                last.then_inc(lg_full, 1)

            def ranks(prv):
                pe.wait_ge(route_step, prv.n * ROUTE + ROUTE)
                dst = RK[:, :, :].rearrange("p s e -> p (s e)")
                pe.matmul(dst, before[:, :], chosen_any[:, :, :].rearrange("p s e -> p (s e)"), start=True, stop=False)
                pe.matmul(dst, ones_bf[:, :], earlier[:, 0:SUB, :].rearrange("p s e -> p (s e)"),
                          start=False, stop=True).then_inc(rk_full, 1)

            def step(cur, nxt, prv):
                heads(cur, range(0, 4))
                if prv:
                    routing_t(prv)
                heads(cur, range(4, 8))
                if prv:
                    routing_logits(prv)
                heads(cur, range(8, 12))
                if nxt:
                    transposes(nxt)
                heads(cur, range(12, 16))
                if prv:
                    ranks(prv)
                if nxt:
                    queries(nxt)
                for h in range(HEADS - LAG, HEADS):
                    values(cur, h)
                if nxt:
                    maxima(nxt)
                output(cur)
                if nxt:
                    maxima_t(nxt)

            transposes(Blk(0, 0))
            queries(Blk(0, 0))
            maxima(Blk(0, 0))
            maxima_t(Blk(0, 0))
            step(Blk(0, 0), Blk(0, 1), None)
            with pe.Fori(0, BLOCKS // 2 - 1, 1) as j:
                step(Blk(j, 1), Blk(j + 1, 0), Blk(j, 0))
                step(Blk(j + 1, 0), Blk(j + 1, 1), Blk(j, 1))
            final = Blk(BLOCKS // 2 - 1, 1)
            step(final, None, Blk(BLOCKS // 2 - 1, 0))
            routing_t(final)
            routing_logits(final)
            ranks(final)
            pe.wait_ge(place_step, BLOCKS * 5)
            pe.matmul(TOTAL, ones_bf[:, :], earlier[:, SUB, :], start=True, stop=True).then_inc(total_full, 1)

        @block.vector
        def _(dve):
            dve.wait_ge(const_set, CONST_SET)
            dve.tensor_copy(iota_f[:, :, :], iota_i[:, :, :]).then_inc(const_f, 1)
            for b in range(BATCHES):
                dve.tensor_copy(tok_f[b][:, :], tok_i[b][:, :]).then_inc(const_f, 1)
            dve.wait_ge(const_f, 1)
            dve.tensor_scalar(region_f[:, :, :], iota_f[:, :, :], float(REGION), None, ALU.mult).then_inc(const_f, 1)
            dve.wait_ge(small_in, 16 * SMALL)
            dve.wait_ge(tanh_done, 1)
            dve.tensor_scalar(bo_row[:, :], bo_row[:, :], tanh_g[:, 0:1], None, ALU.mult).then_inc(gated, 1)
            dve.wait_ge(wo_in, 16)
            dve.tensor_scalar(wo_raw[:, :, :], wo_raw[:, :, :], tanh_g[:, 0:1], None, ALU.mult).then_inc(gated, 1)
            dve.wait_ge(w_hi_done, 1)
            dve.tensor_tensor(wq_lo[:, :, :], wq_raw[:, :, :], wq_hi[:, :, :].bitcast(F32), ALU.subtract).then_inc(w_lo_done, 1)
            dve.wait_ge(w_hi_done, 2)
            dve.tensor_tensor(wo_lo[:, :, :], wo_raw[:, :, :], wo_hi[:, :, :].bitcast(F32), ALU.subtract).then_inc(w_lo_done, 1)
            dve.tensor_copy(wr_parts[:, :, 0, :], wr[:, :, :]).then_inc(wr_done, 1)
            dve.wait_ge(wr_done, 1)
            dve.tensor_tensor(wr_rest[:, 0, :, :], wr[:, :, :], wr_parts[:, :, 0, :], ALU.subtract).then_inc(wr_done, 1)
            dve.wait_ge(wr_done, 2)
            dve.tensor_copy(wr_parts[:, :, 1, :], wr_rest[:, 0, :, :]).then_inc(wr_done, 1)
            dve.wait_ge(wr_done, 3)
            dve.tensor_tensor(wr_rest[:, 1, :, :], wr_rest[:, 0, :, :], wr_parts[:, :, 1, :], ALU.subtract).then_inc(wr_done, 1)
            dve.wait_ge(wr_done, 4)
            dve.tensor_copy(wr_parts[:, :, 2, :], wr_rest[:, 1, :, :]).then_inc(wr_done, 1)
            for b in range(BATCHES):
                dve.wait_ge(ctx_hi, b + 1)
                dve.tensor_tensor(o_lo[:, 0, :], psF[0][:, :], o_hi[:, 0, :].bitcast(F32), ALU.subtract).then_inc(ctx_lo, 1)
                dve.wait_ge(kv_full, b + 1)
                wait(dve, kt_full, b)
                dve.tensor_tensor(kv[:, :], psB[0][:, :], bq_row[:, :], ALU.add).then_inc(kv_done, 1)
                dve.wait_ge(kv_done, b + 1)
                dve.tensor_copy(v_parts[b][:, 0, :], kv[:, :]).then_inc(v_done, 1)
                dve.wait_ge(v_done, b * 5 + 1)
                dve.tensor_tensor(prob[:, 0, :], kv[:, :], v_parts[b][:, 0, :], ALU.subtract).then_inc(v_done, 1)
                dve.wait_ge(v_done, b * 5 + 2)
                dve.tensor_copy(v_parts[b][:, 1, :], prob[:, 0, :]).then_inc(v_done, 1)
                dve.wait_ge(v_done, b * 5 + 3)
                dve.tensor_tensor(prob[:, 1, :], prob[:, 0, :], v_parts[b][:, 1, :], ALU.subtract).then_inc(v_done, 1)
                dve.wait_ge(v_done, b * 5 + 4)
                dve.tensor_copy(v_parts[b][:, 2, :], prob[:, 1, :]).then_inc(v_done, 1)
                dve.wait_ge(kt_hi, b + 1)
                for i in range(PER_CHUNK):
                    r = slice(DK * i, DK * i + DK)
                    last = dve.tensor_tensor(k_lo[b][r, :, i, :], psF[1][r, :].rearrange("p (c k) -> p c k", c=DC),
                                             k_hi[b][r, :, i, :].bitcast(F32), ALU.subtract)
                last.then_inc(kt_lo, 1)

            def ln_stats(n, src, stats, mv, stats_done, mv_done, held):
                for s in range(SUB):
                    dve.bn_stats(stats[:, s, :], src[:, s, :]).then_inc(stats_done, 1)
                dve.wait_ge(stats_done, n * SUB + SUB)
                hold(dve, spare_dve, held_dve, held)
                for s in range(SUB):
                    dve.bn_aggr(mv[:, s, :], stats[:, s, :]).then_inc(mv_done, 1)

            def ln1_stats(nxt):
                dve.wait_ge(x_in[nxt.b], 16 * nxt.q + 16)
                ln_stats(nxt.n, x[nxt.b], stats1, mv1, stats1_done, mv1_done,
                         2 * nxt.n - (0 if nxt.first else 1))

            def ln1(nxt):
                dve.wait_ge(rstd1_done, nxt.n + 1)
                for s in range(SUB):
                    last = dve.tensor_scalar(xn[:, s, :], x[nxt.b][:, s, :], mv1[:, s, 0:1], rstd1[:, s:s + 1], ALU.subtract, ALU.mult)
                last.then_inc(xn_done, 1)

            def ln2_stats(cur):
                dve.wait_ge(f_free, cur.f_output(3) + 1)
                ln_stats(cur.n, x[cur.b], stats2, mv2, stats2_done, mv2_done,
                         2 * cur.n + (1 if cur.last else 2))

            def ln2(prv):
                dve.wait_ge(rstd2_done, prv.n + 1)
                wait(dve, scattered, prv.n * (16 * TOPK * SUB))
                for s in range(SUB):
                    last = dve.tensor_scalar(rows[:, s, 0:D], x[prv.b][:, s, :], mv2[:, s, 0:1], rstd2[:, s:s + 1], ALU.subtract, ALU.mult)
                last.then_inc(xn2_done, 1)

            def halves(nxt):
                for c in range(DC):
                    dve.wait_ge(xt_hi_done, nxt.n * DC + c + 1)
                    dve.tensor_tensor(xt_lo[:, c, :], psF[c % 2][:, :], xt_hi[:, c, :].bitcast(F32), ALU.subtract).then_inc(f_free, 1)

            def queries(nxt):
                for m in range(DC):
                    dve.wait_ge(q_hi_done, nxt.n * DC + m + 1)
                    dve.scalar_tensor_tensor(out=q_lo[:, m, :], in0=psF[m % 2][:, :], scalar=bq_col[:, m:m + 1],
                                             in1=q_hi[:, m, :].bitcast(F32), op0=ALU.add, op1=ALU.subtract).then_inc(f_free, 1)

            def maxima(nxt):
                for s in range(SUB):
                    for c in range(DC):
                        u = s * DC + c
                        dve.wait_ge(f_full, nxt.f_maxima(u) + 1)
                        dve.tensor_reduce(mx[:, s, PER_CHUNK * c:PER_CHUNK * c + PER_CHUNK],
                                          psF[u % 2][:, :].rearrange("p (i k) -> p i k", i=PER_CHUNK), AX_X, ALU.max).then_inc(f_free, 1)
                dve.wait_ge(f_free, nxt.f_maxima(SUB * DC - 1) + 1)
                dve.tensor_copy(mx_parts[:, :, 0:HEADS], mx[:, :, :]).then_inc(mx_step, 1)
                dve.wait_ge(mx_step, nxt.n * 3 + 1)
                dve.tensor_tensor(mx_rest[:, :, :], mx[:, :, :], mx_parts[:, :, 0:HEADS], ALU.subtract).then_inc(mx_step, 1)
                dve.wait_ge(mx_step, nxt.n * 3 + 2)
                dve.tensor_copy(mx_parts[:, :, HEADS:], mx_rest[:, :, :]).then_inc(mx_step, 1)

            def maxima_t(nxt):
                dve.wait_ge(mx_full, nxt.n + 1)
                dve.tensor_copy(mx_t[0:2 * HEADS, :], psM[0:2 * HEADS, 0:BLOCK]).then_inc(mx_t_done, 1)

            def prob_lo(cur, hs):
                for h in hs:
                    c = cur.n * HEADS + h
                    dve.wait_ge(exp_done, c + 1)
                    dve.tensor_tensor(p_lo[:, h % 4, :], prob[:, h % 4, :], p_hi[:, h % 4, :], ALU.subtract).then_inc(p_lo_done, 1)
                    if h % 4 == 2 and h > 2:
                        divide(cur, h // 4 - 1)

            def divide(cur, c):
                k = cur.n * DC + c
                dve.wait_ge(pv_done, cur.n * HEADS + PER_CHUNK * c + PER_CHUNK)
                dve.reciprocal(rden[:, :], psD[:, :]).then_inc(rden_done, 1)
                dve.wait_ge(rden_done, k + 1)
                wait(dve, o_lo_done, k - 1)
                dve.tensor_tensor(o_f[:, c % 2, :], psO[:, :], rden[:, :], ALU.mult).then_inc(o_done, 1)

            def output(cur):
                dve.wait_ge(xb_done, cur.n + 1)
                for s in range(SUB):
                    dve.wait_ge(f_full, cur.f_output(s) + 1)
                    dve.tensor_tensor(x[cur.b][:, s, :], psF[s % 2][:, :], x[cur.b][:, s, :], ALU.add).then_inc(f_free, 1)

            def routing_lo(prv):
                for s in range(SUB):
                    dve.wait_ge(r_hi_done, prv.n * SUB + s + 1)
                    dve.scalar_tensor_tensor(out=r_lo[:, s, :], in0=psF[s % 2][:, :], scalar=X_SCALE, in1=r_hi[:, s, :],
                                             op0=ALU.mult, op1=ALU.subtract).then_inc(f_free, 1)

            def route(prv):
                base = prv.n * ROUTE
                done = [0]

                def link(ins):
                    done[0] += 1
                    ins.then_inc(route_step, 1)

                def after(k):
                    dve.wait_ge(route_step, base + k)

                dve.wait_ge(lg_full, prv.n + 1)
                link(dve.tensor_reduce(lsum[:, :, :], LG[:, :, 0:3 * EXPERTS].rearrange("p s (k e) -> p s e k", k=3), AX_X, ALU.add))
                after(1)
                link(dve.tensor_scalar(logits[:, :, :], lsum[:, :, :], 1.0 / X_SCALE, None, ALU.mult))
                after(2)
                link(dve.tensor_tensor(logits[:, :, :], logits[:, :, :], rb_row[:, :].unsqueeze(1).to_broadcast([P, SUB, EXPERTS]), ALU.add))
                after(3)
                link(dve.tensor_copy(earlier[:, 0, :], earlier[:, SUB, :]))
                for s in range(SUB):
                    link(dve.max(top[:, s, :], logits[:, s, :]))
                after(8)
                link(dve.tensor_tensor(wdiff[:, :], top[:, :, 1], top[:, :, 0], ALU.subtract))
                for s in range(SUB):
                    link(dve.max_index(top_ix[:, s, :], top[:, s, :], logits[:, s, :]))
                after(13)
                link(dve.tensor_copy(pick[:, :, :], top_ix[:, :, 0:TOPK]))
                after(14)
                for k in range(TOPK):
                    link(dve.tensor_tensor(chosen[k][:, :, :], iota_f[:, :, :],
                                           pick[:, :, k:k + 1].to_broadcast([P, SUB, EXPERTS]), ALU.is_equal))
                after(16)
                link(dve.tensor_tensor(chosen_any[:, :, :], chosen[0][:, :, :], chosen[1][:, :, :], ALU.add))
                for s in range(SUB):
                    after(17 + s)
                    link(dve.tensor_tensor(earlier[:, s + 1, :], earlier[:, s, :], chosen_any[:, s, :], ALU.add))
                assert done[0] == ROUTE

            def weights(prv):
                base = prv.n * 6
                dve.wait_ge(wexp_done, prv.n + 1)
                dve.tensor_scalar(wden[:, :], wexp[:, :], 1.0, None, ALU.add).then_inc(meta_done, 1)
                dve.wait_ge(meta_done, base + 1)
                dve.reciprocal(wrec[:, :], wden[:, :]).then_inc(meta_done, 1)
                dve.wait_ge(meta_done, base + 2)
                dve.tensor_scalar(whigh[:, :], wrec[:, :], tanh_g[:, 1:2], None, ALU.mult).then_inc(meta_done, 1)
                dve.wait_ge(meta_done, base + 3)
                dve.tensor_tensor(rows[:, :, W_LOW], whigh[:, :], wexp[:, :], ALU.mult).then_inc(meta_done, 1)
                dve.wait_ge(meta_done, base + 4)
                dve.tensor_tensor(rows[:, :, W_DIFF], whigh[:, :], rows[:, :, W_LOW], ALU.subtract).then_inc(meta_done, 1)
                dve.tensor_copy(rows[:, :, FIRST_EXPERT], pick[:, :, 0])
                dve.tensor_copy(rows[:, :, TOKEN].bitcast(I32), tok_f[prv.b][:, :]).then_inc(meta_done, 1)
                dve.wait_ge(meta_done, base + 6)
                dve.tensor_scalar(tok_f[prv.b][:, :], tok_f[prv.b][:, :], float(BLOCK), None, ALU.add).then_inc(const_f, 1)

            def targets(prv):
                base = prv.n * 5
                dve.wait_ge(rk_full, prv.n + 1)
                dve.tensor_tensor(place[:, :, :], RK[:, :, :], region_f[:, :, :], ALU.add).then_inc(place_step, 1)
                dve.wait_ge(place_step, base + 1)
                for k in range(TOPK):
                    dve.tensor_tensor(place_k[:, k, :, :], place[:, :, :], chosen[k][:, :, :], ALU.mult).then_inc(place_step, 1)
                dve.wait_ge(place_step, base + 3)
                dve.tensor_reduce(place_s[:, :, :], place_k[:, :, :, :], AX_X, ALU.add).then_inc(place_step, 1)
                dve.wait_ge(place_step, base + 4)
                dve.tensor_copy(target[:, :, :], place_s[:, :, :]).then_inc(place_step, 1)

            def step(cur, nxt, prv):
                if prv:
                    ln2(prv)
                prob_lo(cur, range(0, 4))
                if prv:
                    routing_lo(prv)
                if nxt:
                    ln1_stats(nxt)
                prob_lo(cur, range(4, 8))
                if nxt:
                    ln1(nxt)
                prob_lo(cur, range(8, 12))
                if prv:
                    route(prv)
                    weights(prv)
                if nxt:
                    halves(nxt)
                prob_lo(cur, range(12, 16))
                if prv:
                    targets(prv)
                if nxt:
                    queries(nxt)
                divide(cur, DC - 1)
                if nxt:
                    maxima(nxt)
                output(cur)
                if nxt:
                    maxima_t(nxt)
                ln2_stats(cur)

            first, final = Blk(0, 0), Blk(BLOCKS // 2 - 1, 1)
            ln1_stats(first)
            ln1(first)
            halves(first)
            queries(first)
            maxima(first)
            maxima_t(first)
            step(first, Blk(0, 1), None)
            with dve.Fori(0, BLOCKS // 2 - 1, 1) as j:
                step(Blk(j, 1), Blk(j + 1, 0), Blk(j, 0))
                step(Blk(j + 1, 0), Blk(j + 1, 1), Blk(j, 1))
            step(final, None, Blk(BLOCKS // 2 - 1, 0))
            ln2(final)
            routing_lo(final)
            route(final)
            weights(final)
            targets(final)
            dve.wait_ge(total_full, 1)
            dve.tensor_copy(counts[:, :], TOTAL).then_inc(counts_done, 1)


def at(i):
    return bass.ds(i, 1)


class Slot:

    def __init__(self, q, r):
        self.q, self.r, self.s = q + r // RING, r % RING, q * RING + r
        self.half = r % 2

    def next(self):
        return Slot(self.q, self.r + 1)


def experts(nc, A, out, rows_sorted, counts_dram):
    with ExitStack() as ctx:
        def sb(name, shape, dt):
            return ctx.enter_context(nc.sbuf_tensor(name, shape, dt))

        def bank(name):
            return ctx.enter_context(nc.psum_tensor(name, [P, 512], F32))

        def sem(name):
            return ctx.enter_context(nc.semaphore(name))

        w_raw = sb("w_raw", [P, MATS * DC, D], F32)
        w_hi = sb("w_hi", [P, 2, MATS * DC, D], F32R)
        w_lo = sb("w_lo", [P, 2, MATS * DC, D], F32R)
        ident = sb("e_ident", [P, P], F32)
        row_in = [sb(f"row_in{r}", [P, ROW], F32) for r in range(RING)]
        xt_hi, xt_lo = ([sb(f"e_xt_{n}{r}", [P, D], F32R) for r in range(2)] for n in ("hi", "lo"))
        ht_hi, ht_lo = ([sb(f"e_ht_{n}{r}", [P, D], F32R) for r in range(2)] for n in ("hi", "lo"))
        silu = [sb(f"silu{r}", [P, D], F32) for r in range(2)]
        hidden = [sb(f"hidden{r}", [P, D], F32) for r in range(2)]
        y = [sb(f"y{r}", [P, D], F32) for r in range(RING)]
        spare = sb("spare", [1, 2], F32)
        is_first = sb("is_first", [P, RING], F32)
        weight = sb("weight", [P, RING], F32)
        counts = sb("e_counts", [P, EXPERTS], F32)
        MOST = TOKENS // P
        steps_i, steps_f = sb("steps_i", [P, EXPERTS, MOST], I32), sb("steps_f", [P, EXPERTS, MOST], F32)
        over = sb("over", [P, EXPERTS, MOST], F32)
        tiles, ends, ones8, fill_f = (sb(n, [P, EXPERTS], F32) for n in ("tiles", "ends", "ones8", "fill_f"))
        sign = sb("sign", [P, EXPERTS - 1], F32)
        slot_i, eight_i, fill_t = sb("slot_i", [P, SLOTS], I32), sb("eight_i", [P, EXPERTS], I32), sb("fill_t", [P, EXPERTS], I32)
        passed, passed_n = (sb(n, [P, SLOTS, EXPERTS - 1], F32) for n in ("passed", "passed_n"))
        slot_f, expert_f, start_f, parity_f, off_f, row_f, valid_f, first_f = (sb(n, [P, SLOTS], F32) for n in (
            "slot_f", "expert_f", "start_f", "parity_f", "off_f", "row_f", "valid_f", "first_f"))
        row_t, expert_t, first_t, parity_t, other_t, stage_t = (sb(n, [P, SLOTS], I32) for n in (
            "row_t", "expert_t", "first_t", "parity_t", "other_t", "stage_t"))
        blank = sb("blank", [P, ROW], F32)

        psX, psH = bank("psX"), bank("psH")
        psG, psU, psY = ([bank(f"{n}{r}") for r in range(2)] for n in ("psG", "psU", "psY"))

        counts_in, consts, made = sem("counts_in"), sem("e_consts"), sem("made")
        tail_out, filled = sem("tail_out"), sem("filled")
        w_in, w_halves, w_split = sem("w_in"), sem("w_halves"), sem("w_split")
        rows_landed = [sem(f"rows_landed{r}") for r in range(RING)]
        xt_full, xt_hi_done, xt_done = sem("e_xt_full"), sem("e_xt_hi_done"), sem("e_xt_done")
        gate_full, up_full, silu_done, hidden_done = sem("gate_full"), sem("up_full"), sem("silu_done"), sem("hidden_done")
        ht_full, ht_hi_done, ht_done = sem("ht_full"), sem("ht_hi_done"), sem("ht_done")
        y_full, w_step, y_done, added = sem("y_full"), sem("w_step"), sem("y_done"), sem("added")
        held = sem("held")
        CONSTS, MADE = 11, 26
        mats = [A[n] for n in ("we_gate", "we_up", "we_down")]
        LOOPED = (SLOTS - 3) // RING
        assert LOOPED * RING == SLOTS - 3
        FINAL = Slot(0, SLOTS - 1)

        block = ctx.enter_context(nc.Block())

        @block.sync
        def _(sp):
            sp.dma_start(counts[:, :], counts_dram).then_inc(counts_in, 16)
            sp.wait_ge(consts, CONSTS)
            sp.dma_start(out[TOKENS:TOKENS + P, :], blank[:, 0:D]).then_inc(tail_out, 16)
            sp.dma_start(rows_sorted[DUMMY:DUMMY + P, :], blank[:, :]).then_inc(filled, 16)
            sp.wait_ge(made, MADE)
            for e in range(EXPERTS):
                r = sp.value_load(fill_t[0:1, e:e + 1], min_val=e * REGION, max_val=e * REGION + TOKENS)
                sp.dma_start(rows_sorted[bass.ds(r, P), :], blank[:, :]).then_inc(filled, 16)
            sp.wait_ge(filled, 16 * (EXPERTS + 1))

            def load(k):
                row = sp.value_load(row_t[0:1, at(k.s)], min_val=0, max_val=DUMMY)
                wait(sp, added, (k.s - RING) * 16 + 16)
                sp.dma_start(row_in[k.r][:, :], rows_sorted[bass.ds(row, P), :]).then_inc(rows_landed[k.r], 16)

            for r in range(RING):
                load(Slot(0, r))
            with sp.Fori(1, SLOTS // RING, 1) as i:
                for r in range(RING):
                    load(Slot(i, r))
            for s in range(SLOTS // RING * RING, SLOTS):
                load(Slot(0, s))
            sp.wait_ge(tail_out, 16)

        @block.gpsimd
        def _(pool):
            def stage(e):
                for m in range(MATS):
                    pool.dma_start(w_raw[:, m * DC:m * DC + DC, :],
                                   mats[m][at(e)].rearrange("a (c p) n -> p (a c) n", p=P)).then_inc(w_in, 16)

            def split(parity, n):
                pool.wait_ge(w_in, 16 * MATS * (n + 1))
                pool.tensor_copy(w_hi[:, at(parity), :, :].rearrange("p a c n -> p (a c n)"),
                                 w_raw[:, :, :].rearrange("p c n -> p (c n)")).then_inc(w_halves, 1)
                pool.wait_ge(w_halves, n + 1)
                pool.tensor_tensor(w_lo[:, at(parity), :, :].rearrange("p a c n -> p (a c n)"),
                                   w_raw[:, :, :].rearrange("p c n -> p (c n)"),
                                   w_hi[:, at(parity), :, :].rearrange("p a c n -> p (a c n)").bitcast(F32),
                                   ALU.subtract).then_inc(w_split, 1)
                pool.wait_ge(w_split, n + 1)

            stage(0)
            for t in (ident, blank, spare):
                pool.memset(t[:, :], 0.0).then_inc(consts, 1)
            pool.memset(ones8[:, :], 1.0).then_inc(consts, 1)
            pool.memset(sign[:, :], 1.0).then_inc(consts, 1)
            pool.iota(slot_i[:, :], pattern=[[1, SLOTS]], base=0, channel_multiplier=0).then_inc(consts, 1)
            pool.iota(steps_i[:, :, :], pattern=[[0, EXPERTS], [P, MOST]], base=0, channel_multiplier=0).then_inc(consts, 1)
            pool.iota(eight_i[:, :], pattern=[[REGION, EXPERTS]], base=0, channel_multiplier=0).then_inc(consts, 1)
            pool.wait_ge(consts, 8)
            pool.iota(blank[:, TOKEN:TOKEN + 1].bitcast(I32), pattern=[[0, 1]], base=TOKENS, channel_multiplier=1).then_inc(consts, 1)
            pool.memset(sign[:, 1::2], -1.0).then_inc(consts, 1)
            pool.affine_select(out=ident[:, :], in_=ident[:, :], compare_op=ALU.not_equal, fill=1.0, base=0,
                               pattern=[[-1, P]], channel_multiplier=1).then_inc(consts, 1)
            split(0, 0)
            stage(1)
            pool.wait_ge(made, MADE)
            pool.wait_ge(tail_out, 16)

            def slot(k):
                first = pool.value_load(first_t[0:1, at(k.s)], min_val=0, max_val=1)
                e = pool.value_load(expert_t[0:1, at(k.s)], min_val=0, max_val=EXPERTS - 1)
                other = pool.value_load(other_t[0:1, at(k.s)], min_val=0, max_val=1)
                after = pool.value_load(stage_t[0:1, at(k.s)], min_val=0, max_val=EXPERTS - 1)
                with pool.If(first > 0):
                    wait(pool, y_full, k.s)
                    split(other, e + 1)
                    stage(after)
                pool.wait_ge(y_done, k.s + 1)
                wait(pool, added, k.s * 16)
                hold(pool, spare, held, k.s)
                pool.indirect_dma_start(
                    out=out, out_offset=bass.IndirectOffsetOnAxis(ap=row_in[k.r][:, TOKEN:TOKEN + 1].bitcast(U32), axis=0),
                    in_=y[k.r][:, :], in_offset=None, bounds_check=TOKENS + P - 1, oob_is_err=True,
                    compute_op=ALU.add).then_inc(added, 16)

            slot(Slot(0, 0))
            for u in range(RING):
                slot(Slot(0, 1 + u))
            with pool.Fori(1, LOOPED, 1) as i:
                for u in range(RING):
                    slot(Slot(i, 1 + u))
            for s in range(SLOTS - 2, SLOTS):
                slot(Slot(0, s))
            pool.wait_ge(added, 16 * SLOTS)
            pool.wait_ge(w_in, 16 * MATS * EXPERTS)

        @block.scalar
        def _(act):
            def xt(k):
                act.wait_ge(xt_full, k.s + 1)
                wait(act, up_full, k.s - 1)
                act.activation(xt_hi[k.half][:, :], psX[:, :], ACT.Copy).then_inc(xt_hi_done, 1)

            def ht(k):
                act.wait_ge(ht_full, k.s + 1)
                wait(act, y_full, k.s - 1)
                act.activation(ht_hi[k.half][:, :], psH[:, :], ACT.Copy).then_inc(ht_hi_done, 1)

            def gate(k):
                act.wait_ge(gate_full, k.s + 1)
                wait(act, hidden_done, k.s - 1)
                act.activation(silu[k.half][:, :], psG[k.half][:, :], ACT.Silu).then_inc(silu_done, 1)

            def result(k):
                act.wait_ge(y_full, k.s + 1)
                act.wait_ge(w_step, k.s * 2 + 2)
                wait(act, added, (k.s - RING) * 16 + 16)
                act.activation(y[k.r][:, :], psY[k.half][:, :], ACT.Copy, scale=weight[:, k.r:k.r + 1]).then_inc(y_done, 1)

            def body(k):
                xt(k.next())
                ht(k.prev)
                gate(k)
                result(k.prev)

            xt(Slot(0, 0))
            xt(Slot(0, 1))
            gate(Slot(0, 0))
            for u in range(RING):
                body(with_prev(0, 1 + u))
            with act.Fori(1, LOOPED, 1) as i:
                for u in range(RING):
                    body(with_prev(i, 1 + u))
            body(with_prev(0, SLOTS - 2))
            ht(Slot(0, SLOTS - 2))
            gate(FINAL)
            result(Slot(0, SLOTS - 2))
            ht(FINAL)
            result(FINAL)

        @block.tensor
        def _(pe):
            def split3(dst, hi, lo, par, m):
                for c in range(DC):
                    wh = w_hi[:, at(par), m * DC + c, :].rearrange("p a n -> p (a n)")
                    wl = w_lo[:, at(par), m * DC + c, :].rearrange("p a n -> p (a n)")
                    cs = slice(c * P, c * P + P)
                    pe.matmul(dst[:, :], hi[:, cs], wh, start=c == 0, stop=False)
                    pe.matmul(dst[:, :], hi[:, cs], wl, start=False, stop=False)
                    last = pe.matmul(dst[:, :], lo[:, cs], wh, start=False, stop=c == DC - 1)
                return last

            def xt(k):
                pe.wait_ge(rows_landed[k.r], k.q * 16 + 16)
                wait(pe, xt_done, k.s)
                for c in range(DC):
                    last = pe.transpose(psX[:, c * P:c * P + P], row_in[k.r][:, c * P:c * P + P], ident[:, :])
                last.then_inc(xt_full, 1)

            def ht(k):
                pe.wait_ge(hidden_done, k.s + 1)
                wait(pe, ht_done, k.s)
                for c in range(DC):
                    last = pe.transpose(psH[:, c * P:c * P + P], hidden[k.half][:, c * P:c * P + P], ident[:, :])
                last.then_inc(ht_full, 1)

            def gate_up(k):
                e = pe.value_load(expert_t[0:1, at(k.s)], min_val=0, max_val=EXPERTS - 1)
                par = pe.value_load(parity_t[0:1, at(k.s)], min_val=0, max_val=1)
                pe.wait_ge(w_split, e + 1)
                pe.wait_ge(xt_done, k.s + 1)
                wait(pe, hidden_done, k.s - 1)
                split3(psG[k.half], xt_hi[k.half], xt_lo[k.half], par, 0).then_inc(gate_full, 1)
                split3(psU[k.half], xt_hi[k.half], xt_lo[k.half], par, 1).then_inc(up_full, 1)

            def down(k):
                par = pe.value_load(parity_t[0:1, at(k.s)], min_val=0, max_val=1)
                pe.wait_ge(ht_done, k.s + 1)
                wait(pe, y_done, k.s - 1)
                split3(psY[k.half], ht_hi[k.half], ht_lo[k.half], par, 2).then_inc(y_full, 1)

            def body(k):
                xt(k.next())
                ht(k.prev)
                gate_up(k)
                down(k.prev)

            pe.wait_ge(consts, CONSTS)
            pe.wait_ge(made, MADE)
            xt(Slot(0, 0))
            xt(Slot(0, 1))
            gate_up(Slot(0, 0))
            for u in range(RING):
                body(with_prev(0, 1 + u))
            with pe.Fori(1, LOOPED, 1) as i:
                for u in range(RING):
                    body(with_prev(i, 1 + u))
            body(with_prev(0, SLOTS - 2))
            ht(Slot(0, SLOTS - 2))
            gate_up(FINAL)
            down(Slot(0, SLOTS - 2))
            ht(FINAL)
            down(FINAL)

        @block.vector
        def _(dve):
            done = [0]

            def link(ins):
                done[0] += 1
                ins.then_inc(made, 1)
                dve.wait_ge(made, done[0])

            by_step = [P, EXPERTS, MOST]
            by_slot = [P, SLOTS, EXPERTS - 1]
            dve.wait_ge(counts_in, 16)
            dve.wait_ge(consts, CONSTS)
            link(dve.tensor_copy(steps_f[:, :, :], steps_i[:, :, :]))
            link(dve.tensor_copy(slot_f[:, :], slot_i[:, :]))
            link(dve.tensor_copy(fill_f[:, :], eight_i[:, :]))
            link(dve.tensor_tensor(over[:, :, :], counts[:, :].unsqueeze(2).to_broadcast(by_step), steps_f[:, :, :], ALU.is_gt))
            link(dve.tensor_reduce(tiles[:, :], over[:, :, :], AX_X, ALU.add))
            link(dve.tensor_scalar(tiles[:, :], tiles[:, :], 1.0, None, ALU.max))
            link(dve.tensor_tensor_scan(ends[:, :], ones8[:, :], tiles[:, :], 0.0, ALU.mult, ALU.add))
            link(dve.tensor_tensor(passed[:, :, :], slot_f[:, :].unsqueeze(2).to_broadcast(by_slot),
                                   ends[:, 0:EXPERTS - 1].unsqueeze(1).to_broadcast(by_slot), ALU.is_ge))
            link(dve.tensor_reduce(expert_f[:, :], passed[:, :, :], AX_X, ALU.add))
            link(dve.tensor_tensor(passed_n[:, :, :], passed[:, :, :], tiles[:, 0:EXPERTS - 1].unsqueeze(1).to_broadcast(by_slot), ALU.mult))
            link(dve.tensor_reduce(start_f[:, :], passed_n[:, :, :], AX_X, ALU.add))
            link(dve.tensor_tensor(passed_n[:, :, :], passed[:, :, :], sign[:, :].unsqueeze(1).to_broadcast(by_slot), ALU.mult))
            link(dve.tensor_reduce(parity_f[:, :], passed_n[:, :, :], AX_X, ALU.add))
            link(dve.tensor_tensor(off_f[:, :], slot_f[:, :], start_f[:, :], ALU.subtract))
            link(dve.tensor_scalar(row_f[:, :], off_f[:, :], float(P), None, ALU.mult))
            link(dve.scalar_tensor_tensor(out=row_f[:, :], in0=expert_f[:, :], scalar=float(REGION), in1=row_f[:, :], op0=ALU.mult, op1=ALU.add))
            link(dve.tensor_scalar(valid_f[:, :], slot_f[:, :], ends[:, EXPERTS - 1:EXPERTS], None, ALU.is_lt))
            link(dve.scalar_tensor_tensor(out=row_f[:, :], in0=row_f[:, :], scalar=-float(DUMMY), in1=valid_f[:, :], op0=ALU.add, op1=ALU.mult))
            link(dve.tensor_scalar(row_t[:, :], row_f[:, :], float(DUMMY), None, ALU.add))
            link(dve.scalar_tensor_tensor(out=first_f[:, :], in0=off_f[:, :], scalar=0.0, in1=valid_f[:, :], op0=ALU.is_equal, op1=ALU.mult))
            link(dve.scalar_tensor_tensor(out=first_t[:, :], in0=expert_f[:, :], scalar=float(EXPERTS - 1), in1=first_f[:, :], op0=ALU.is_lt, op1=ALU.mult))
            link(dve.tensor_copy(expert_t[:, :], expert_f[:, :]))
            link(dve.tensor_copy(parity_t[:, :], parity_f[:, :]))
            link(dve.tensor_scalar(other_t[:, :], parity_f[:, :], -1.0, 1.0, ALU.mult, ALU.add))
            link(dve.tensor_scalar(stage_t[:, :], expert_f[:, :], 2.0, float(EXPERTS - 1), ALU.add, ALU.min))
            link(dve.tensor_tensor(fill_t[:, :], fill_f[:, :], counts[:, :], ALU.add))
            assert done[0] == MADE

            def xt(k):
                dve.wait_ge(xt_hi_done, k.s + 1)
                dve.tensor_tensor(xt_lo[k.half][:, :], psX[:, :], xt_hi[k.half][:, :].bitcast(F32), ALU.subtract).then_inc(xt_done, 1)

            def ht(k):
                dve.wait_ge(ht_hi_done, k.s + 1)
                dve.tensor_tensor(ht_lo[k.half][:, :], psH[:, :], ht_hi[k.half][:, :].bitcast(F32), ALU.subtract).then_inc(ht_done, 1)

            def combine(k):
                dve.wait_ge(rows_landed[k.r], k.q * 16 + 16)
                wait(dve, y_done, k.s - RING + 1)
                dve.tensor_tensor(is_first[:, k.r:k.r + 1], row_in[k.r][:, FIRST_EXPERT:FIRST_EXPERT + 1],
                                  expert_f[:, at(k.s)], ALU.is_equal).then_inc(w_step, 1)
                dve.wait_ge(w_step, k.s * 2 + 1)
                dve.scalar_tensor_tensor(out=weight[:, k.r:k.r + 1], in0=is_first[:, k.r:k.r + 1],
                                         scalar=row_in[k.r][:, W_DIFF:W_DIFF + 1], in1=row_in[k.r][:, W_LOW:W_LOW + 1],
                                         op0=ALU.mult, op1=ALU.add).then_inc(w_step, 1)

            def hide(k):
                dve.wait_ge(silu_done, k.s + 1)
                dve.wait_ge(up_full, k.s + 1)
                wait(dve, ht_full, k.s - 1)
                dve.tensor_tensor(hidden[k.half][:, :], psU[k.half][:, :], silu[k.half][:, :], ALU.mult).then_inc(hidden_done, 1)

            def body(k):
                xt(k.next())
                combine(k)
                ht(k.prev)
                hide(k)

            xt(Slot(0, 0))
            xt(Slot(0, 1))
            combine(Slot(0, 0))
            hide(Slot(0, 0))
            for u in range(RING):
                body(with_prev(0, 1 + u))
            with dve.Fori(1, LOOPED, 1) as i:
                for u in range(RING):
                    body(with_prev(i, 1 + u))
            body(with_prev(0, SLOTS - 2))
            combine(FINAL)
            ht(Slot(0, SLOTS - 2))
            hide(FINAL)
            ht(FINAL)


def with_prev(q, r):
    k = Slot(q, r)
    k.prev = Slot(q, r - 1)
    return k


def build(nc, A, out):
    rows_sorted = nc.dram_tensor("rows_sorted", [SORTED_ROWS, ROW], F32).ap()
    counts_dram = nc.dram_tensor("counts_kept", [P, EXPERTS], F32).ap()
    attention_and_routing(nc, A, out, rows_sorted, counts_dram)
    experts(nc, A, out, rows_sorted, counts_dram)


_INS = {"x": "x", "ctx": "ctx_1024", "g_xattn": "g_xattn", "g_ffn": "g_ffn", "Wq": "L0_xattn_Wq", "bq": "L0_xattn_bq",
        "Wo": "L0_xattn_Wo", "bo": "L0_xattn_bo", "router_w": "L0_ffn_router_w", "router_b": "L0_ffn_router_b",
        "we_gate": "L0_ffn_we_gate", "we_up": "L0_ffn_we_up", "we_down": "L0_ffn_we_down"}


def kernel(**inputs):
    import concourse.bacc as bacc
    from concourse.bass_utils import run_bass_kernel_spmd

    nc = bacc.Bacc("TRN2", target_bir_lowering=False, num_devices=1)
    arrays, args = {}, {}
    for short, name in _INS.items():
        a = np.ascontiguousarray(inputs[name])
        arrays[f"in_{short}"] = a
        args[short] = nc.dram_tensor(f"in_{short}", a.shape, mybir.dt.from_np(a.dtype), kind="ExternalInput").ap()
    out = nc.dram_tensor("out_rows", [TOKENS + P, D], F32, kind="ExternalOutput").ap()
    build(nc, args, out)
    r = run_bass_kernel_spmd(nc, [arrays], core_ids=[0])
    return r.results[0]["out_rows"][:TOKENS].reshape(BATCHES, SEQ, D)
```

```python
import numpy as np
import concourse.bass as bass
from concourse import mybir
from contextlib import ExitStack

F32 = mybir.dt.float32
F32R = mybir.dt.float32r
F16 = mybir.dt.float16
BF16 = mybir.dt.bfloat16
I32 = mybir.dt.int32
U32 = mybir.dt.uint32
ALU = mybir.AluOpType
ACT = mybir.ActivationFunctionType
AX_X = mybir.AxisListType.X

P = 128
BATCHES, SEQ, D = 2, 2048, 512
TOKENS = BATCHES * SEQ
DC = D // P
HEADS, DK, KEYS = 16, 32, 128
PER_CHUNK = P // DK
BLOCK = 512
SUB = BLOCK // P
BLOCKS = TOKENS // BLOCK
LAST = BLOCKS - 1
EXPERTS, TOPK = 8, 2
EPS = 1e-5
HELD = 7
HELD_F = 3
LAG = 4
SUMS_T = {9: 0, 13: 1}
INVERSES_T = {10: 0, 14: 1}
ROUTING_T = {5: 0, 6: 1, 7: 2, 8: 3}
ROUTE = {10: 0, 11: 1, 12: 2}
TRANSPOSES = {10: 0, 11: 1, 12: 2, 13: 3}
QUERIES = {15: 0}
ROW = D + 8
W_DIFF, W_LOW, FIRST_EXPERT, TOKEN = D, D + 1, D + 2, D + 3
REGION = TOKENS + P
DUMMY = EXPERTS * REGION
SORTED_ROWS = DUMMY + P
SLOTS = TOKENS * TOPK // P + EXPERTS - 1
SLOTS_PAD = SLOTS + 1
RING = 4
MATS = 3
PROB_SCALE = 4096.0
X_SCALE = 2048.0


def wait(eng, sem, value):
    if isinstance(value, int) and value <= 0:
        return
    eng.wait_ge(sem, value)


def hold(eng, spare, held, n):
    wait(eng, held, n)
    eng.tensor_tensor(spare[0:1, 0:1], spare[0:1, 1:2], spare[0:1, 1:2], ALU.add).then_inc(held, 1)


class Blk:

    def __init__(self, q, b):
        self.q, self.b, self.n = q, b, q * BATCHES + b
        self.first = isinstance(self.n, int) and self.n == 0
        self.last = isinstance(self.n, int) and self.n == LAST

    def f_transposes(self, u):
        return self.n * 16 + (u if self.first else u - 8)

    def f_queries(self, u):
        return self.f_transposes(u + 4)

    def f_output(self, u):
        return self.n * 16 + (8 if self.last else 16) + u

    def f_routing(self, u):
        return self.n * 16 + (12 if self.last else 20) + u

    def slot_free(self, h):
        return self.n * HEADS + (0 if h < HELD else h - HELD + 1)

    def low(self, h):
        return self.n * (HEADS // 2) + h // 2 + 1


class Shared:

    def __init__(self, nc, ctx):
        def sb(name, shape, dt):
            return ctx.enter_context(nc.sbuf_tensor(name, shape, dt))

        with ExitStack() as before:
            self.wq_hi, self.wq_lo, self.xt_hi = (
                before.enter_context(nc.sbuf_tensor(n, [P, DC, D], F32R)) for n in ("wq_hi", "wq_lo", "xt_hi"))
        self.w_raw = sb("w_raw", [P, MATS * DC, D], F32)
        self.blank = sb("blank", [P, ROW], F32)
        self.fill_t = sb("fill_t", [P, EXPERTS], I32)
        self.expert_f = sb("expert_f", [P, SLOTS], F32)
        self.row_t, self.expert_t, self.first_t, self.parity_t, self.other_t, self.stage_t = (
            sb(n, [P, SLOTS], I32) for n in ("row_t", "expert_t", "first_t", "parity_t", "other_t", "stage_t"))
        self.w_in = [ctx.enter_context(nc.semaphore(f"w_in{m}")) for m in range(MATS)]


def stage(pool, A, S, e):
    for m, name in enumerate(("we_gate", "we_up", "we_down")):
        pool.dma_start(S.w_raw[:, m * DC:m * DC + DC, :],
                       A[name][at(e)].rearrange("a (c p) n -> p (a c) n", p=P)).then_inc(S.w_in[m], 16)


def attention_and_routing(nc, A, out, rows_sorted, S):
    with ExitStack() as ctx:
        def sb(name, shape, dt):
            return ctx.enter_context(nc.sbuf_tensor(name, shape, dt))

        def bank(name, dt=F32, n=512):
            return ctx.enter_context(nc.psum_tensor(name, [P, n], dt))

        def sem(name):
            return ctx.enter_context(nc.semaphore(name))

        wq_hi, wq_lo, xt_hi = S.wq_hi, S.wq_lo, S.xt_hi
        wo_hi, wo_lo = sb("wo_hi", [P, DC, D], F32R), sb("wo_lo", [P, DC, D], F32R)
        k_hi = [sb(f"k_hi{b}", [P, DC, PER_CHUNK, KEYS], F32R) for b in range(BATCHES)]
        k_lo = [sb(f"k_lo{b}", [P, DC, PER_CHUNK, KEYS], F32R) for b in range(BATCHES)]
        v_parts = [sb(f"v_parts{b}", [P, 3, D], BF16) for b in range(BATCHES)]
        ident = sb("ident", [P, P], F32)
        ident_bf = sb("ident_bf", [P, P], BF16)
        ones_bf = sb("ones_bf", [P, P], BF16)
        before = sb("before", [P, P], BF16)
        minus_head = sb("minus_head", [P, HEADS, KEYS], BF16)
        bq_col = sb("bq_col", [P, DC], F32)
        bq_row = sb("bq_row", [P, D], F32)
        bo_row = sb("bo_row", [P, D], F32)
        rb_row = sb("rb_row", [P, EXPERTS], F32)
        wr = sb("wr", [P, DC, EXPERTS], F32)
        wr_rest = sb("wr_rest", [P, 2, DC, EXPERTS], F32)
        wr_parts = sb("wr_parts", [P, DC, 3, EXPERTS], BF16)
        gates = sb("gates", [P, 2], F32)
        tanh_g = sb("tanh_g", [P, 2], F32)
        minus_half = sb("minus_half", [P, SUB], F32)
        eps = sb("eps", [P, SUB], F32)
        spare_pool, spare_dve = sb("spare_pool", [1, 2], F32), sb("spare_dve", [1, 2], F32)
        exp_bias = sb("exp_bias", [P, 1], F32)
        iota_i = sb("iota_i", [P, SUB, EXPERTS], I32)
        iota_f = sb("iota_f", [P, SUB, EXPERTS], F32)
        region_f = sb("region_f", [P, SUB, EXPERTS], F32)
        tok_i = [sb(f"tok_i{b}", [P, SUB], I32) for b in range(BATCHES)]
        tok_f = [sb(f"tok_f{b}", [P, SUB], F32) for b in range(BATCHES)]
        x = [sb(f"x{b}", [P, SUB, D], F32) for b in range(BATCHES)]
        xn = sb("xn", [P, SUB, D], F32)
        xt_lo = sb("xt_lo", [P, DC, BLOCK], F32R)
        q_hi, q_lo = sb("q_hi", [P, DC, BLOCK], F32R), sb("q_lo", [P, DC, BLOCK], F32R)
        o_hi, o_lo = sb("o_hi", [P, DC, BLOCK], F32R), sb("o_lo", [P, DC, BLOCK], F32R)
        stats1, mv1 = sb("stats1", [P, SUB, 6], F32), sb("mv1", [P, SUB, 2], F32)
        stats2, mv2 = sb("stats2", [P, SUB, 6], F32), sb("mv2", [P, SUB, 2], F32)
        var1, rstd1 = sb("var1", [P, SUB], F32), sb("rstd1", [P, SUB], F32)
        var2, rstd2 = sb("var2", [P, SUB], F32), sb("rstd2", [P, SUB], F32)
        mx = sb("mx", [P, SUB, HEADS], F32)
        mx_rest = sb("mx_rest", [P, SUB, HEADS], F32)
        mx_parts = sb("mx_parts", [P, SUB, 2 * HEADS], BF16)
        mx_t = sb("mx_t", [P, BLOCK], BF16)
        prob = sb("prob", [P, HELD_F, BLOCK], F32)
        p_hi, p_lo = sb("p_hi", [P, HELD, BLOCK], F16), sb("p_lo", [P, HELD, BLOCK], F16)
        sums = sb("sums", [P, BLOCK], F32)
        o_raw = sb("o_raw", [P, BLOCK], F32)
        inverses = sb("inverses", [P, SUB, PER_CHUNK], F32)
        o_f = sb("o_f", [P, 2, BLOCK], F32)
        rows = sb("rows", [P, SUB, ROW], F32)
        r_hi, r_lo = sb("r_hi", [P, SUB, D], F16), sb("r_lo", [P, SUB, D], F16)
        lsum = sb("lsum", [P, SUB, EXPERTS], F32)
        logits = sb("logits", [P, SUB, EXPERTS], F32)
        top = sb("top", [P, SUB, 8], F32)
        top_ix = sb("top_ix", [P, SUB, 8], U32)
        pick = sb("pick", [P, SUB, TOPK], F32)
        chosen = [sb(f"chosen{k}", [P, SUB, EXPERTS], F32) for k in range(TOPK)]
        chosen_any = sb("chosen_any", [P, SUB, EXPERTS], BF16)
        earlier = sb("earlier", [P, SUB + 1, EXPERTS], BF16)
        wdiff, wexp, wden, wrec = (sb(n, [P, SUB], F32) for n in ("wdiff", "wexp", "wden", "wrec"))
        whigh = sb("whigh", [P, SUB], F32)
        place = sb("place", [P, SUB, EXPERTS], F32)
        place_k = sb("place_k", [P, TOPK, SUB, EXPERTS], F32)
        place_s = sb("place_s", [P, TOPK, SUB], F32)
        target = sb("target", [P, TOPK, SUB], I32)
        counts = sb("counts", [P, EXPERTS], F32)

        MOST = TOKENS // P
        steps_i = sb("steps_i", [P, EXPERTS, MOST], I32)
        slot_i, eight_i = sb("slot_i", [P, SLOTS], I32), sb("eight_i", [P, EXPERTS], I32)
        tiles, ends, ones8, fill_f = (sb(n, [P, EXPERTS], F32) for n in ("tiles", "ends", "ones8", "fill_f"))
        sign = sb("sign", [P, EXPERTS - 1], F32)
        passed, passed_n = (xn[:, k, 0:SLOTS * (EXPERTS - 1)].rearrange("p (s e) -> p s e", e=EXPERTS - 1) for k in (0, 1))
        steps_f, over = (xn[:, 2, k * D // 2:(k + 1) * D // 2].rearrange("p (e m) -> p e m", e=EXPERTS) for k in (0, 1))
        slot_f, start_f, parity_f, off_f, row_f, valid_f = (xn[:, 3, k * SLOTS:(k + 1) * SLOTS] for k in range(6))
        first_f = sb("first_f", [P, SLOTS], F32)
        blank, fill_t, expert_f, row_t, expert_t, first_t, parity_t, other_t, stage_t = (
            S.blank, S.fill_t, S.expert_f, S.row_t, S.expert_t, S.first_t, S.parity_t, S.other_t, S.stage_t)
        tail_out, filled, sched_set, made = sem("tail_out"), sem("filled"), sem("sched_set"), sem("made")
        SCHED_SET, MADE, FILL_MADE = 8, 27, 3

        psF = [bank(f"psF{i}") for i in range(2)]
        psB = [bank(f"psB{i}") for i in range(2)]
        psO, psD = bank("psO"), bank("psD")
        ps_max, psL = bank("ps_max"), bank("psL")
        psM = psL[:, 0:256].bitcast(BF16)
        LG = psL[:, 256:256 + SUB * 32].rearrange("p (s w) -> p s w", w=32)
        RK = psL[:, 384:384 + SUB * EXPERTS].rearrange("p (s e) -> p s e", e=EXPERTS)
        TOTAL = psL[:, 448:448 + EXPERTS]


        small_in, wq_in, wo_in, ctx_in = sem("small_in"), sem("wq_in"), sem("wo_in"), sem("ctx_in")
        const_set, const_cut, const_f = sem("const_set"), sem("const_cut"), sem("const_f")
        tanh_done, gated = sem("tanh_done"), sem("gated")
        w_hi_done, w_lo_done = sem("w_hi_done"), sem("w_lo_done")
        wr_done = sem("wr_done")
        ctx_t, ctx_hi, ctx_lo = sem("ctx_t"), sem("ctx_hi"), sem("ctx_lo")
        kv_full, kv_done, v_done = sem("kv_full"), sem("kv_done"), sem("v_done")
        kt_full, kt_hi, kt_lo = sem("kt_full"), sem("kt_hi"), sem("kt_lo")
        held_dve, held_pool = sem("held_dve"), sem("held_pool")
        x_in = [sem(f"x_in{b}") for b in range(BATCHES)]
        x2_out = [sem(f"x2_out{b}") for b in range(BATCHES)]
        stats1_done, mv1_done, var1_done, rstd1_done = (sem(n) for n in ("stats1_done", "mv1_done", "var1_done", "rstd1_done"))
        stats2_done, mv2_done, var2_done, rstd2_done = (sem(n) for n in ("stats2_done", "mv2_done", "var2_done", "rstd2_done"))
        xn_done, xb_done, xn2_done = sem("xn_done"), sem("xb_done"), sem("xn2_done")
        f_full, f_free = sem("f_full"), sem("f_free")
        m_full, m_free = sem("m_full"), sem("m_free")
        xt_hi_done, q_hi_done, r_hi_done = sem("xt_hi_done"), sem("q_hi_done"), sem("r_hi_done")
        mx_step, mx_full, mx_t_done = sem("mx_step"), sem("mx_full"), sem("mx_t_done")
        b_full, exp_done, p_lo_even, p_lo_odd, pv_done = (sem(n) for n in ("b_full", "exp_done", "p_lo_even", "p_lo_odd", "pv_done"))
        copied, sums_t_full, inv_done, inv_t_full = sem("copied"), sem("sums_t_full"), sem("inv_done"), sem("inv_t_full")
        o_done, o_hi_done, o_lo_done = (sem(n) for n in ("o_done", "o_hi_done", "o_lo_done"))
        lg_full, route_step, wexp_done, meta_done = sem("lg_full"), sem("route_step"), sem("wexp_done"), sem("meta_done")
        rk_full, place_step, scattered = sem("rk_full"), sem("place_step"), sem("scattered")
        total_full = sem("total_full")

        wq_raw, wo_raw, ctx_raw, kv = xn, x[1], o_f, sums
        SMALL = 7
        CONST_SET, CONST_CUT = 22, 5
        PAIRS = SUB * DC // 2
        LINKS = 4 + 4 + 4 + 1 + 4 + 4
        x_rows = [A["x"][b].rearrange("(q s p) d -> q p s d", p=P, s=SUB) for b in range(BATCHES)]
        out_rows = [out[b * SEQ:(b + 1) * SEQ, :].rearrange("(q s p) d -> q p s d", p=P, s=SUB) for b in range(BATCHES)]

        block = ctx.enter_context(nc.Block())

        @block.sync
        def _(sp):
            for k, dst, src in (
                ("small", bq_col[:, :], A["bq"].rearrange("(c p) -> p c", p=P)),
                ("small", bq_row[:, :], A["bq"].partition_broadcast(P)),
                ("small", bo_row[:, :], A["bo"].partition_broadcast(P)),
                ("small", rb_row[:, :], A["router_b"].partition_broadcast(P)),
                ("small", wr[:, :, :], A["router_w"].rearrange("(c p) e -> p c e", p=P)),
                ("small", gates[:, 0:1], A["g_xattn"].partition_broadcast(P)),
                ("small", gates[:, 1:2], A["g_ffn"].partition_broadcast(P)),
            ):
                with nc.allow_non_contiguous_dma(reason="a bias by partition"):
                    sp.dma_start(dst, src).then_inc(small_in, 16)
            sp.dma_start(ctx_raw[:, :, :], A["ctx"].rearrange("b p d -> p b d")).then_inc(ctx_in, 16)
            sp.dma_start(wq_raw[:, :, :], A["Wq"].rearrange("(c p) n -> p c n", p=P)).then_inc(wq_in, 16)
            sp.dma_start(wo_raw[:, :, :], A["Wo"].rearrange("(c p) n -> p c n", p=P)).then_inc(wo_in, 16)

            def load_x(nxt):
                if isinstance(nxt.n, int) and nxt.n == 1:
                    sp.wait_ge(w_lo_done, 2)
                elif not nxt.first:
                    sp.wait_ge(x2_out[nxt.b], 16 * nxt.q)
                    sp.wait_ge(xn2_done, nxt.n - 1)
                sp.dma_start(x[nxt.b][:, :, :], x_rows[nxt.b][at(nxt.q)].squeeze(0)).then_inc(x_in[nxt.b], 16)

            def store_x2(cur):
                sp.wait_ge(f_free, cur.f_output(3) + 1)
                sp.dma_start(out_rows[cur.b][at(cur.q)].squeeze(0), x[cur.b][:, :, :]).then_inc(x2_out[cur.b], 16)

            def step(cur, nxt):
                if nxt:
                    load_x(nxt)
                store_x2(cur)

            load_x(Blk(0, 0))
            sp.wait_ge(sched_set, SCHED_SET)
            sp.dma_start(out[TOKENS:TOKENS + P, :], blank[:, 0:D]).then_inc(tail_out, 16)
            sp.dma_start(rows_sorted[DUMMY:DUMMY + P, :], blank[:, :]).then_inc(filled, 16)
            step(Blk(0, 0), Blk(0, 1))
            with sp.Fori(0, BLOCKS // 2 - 1, 1) as j:
                step(Blk(j, 1), Blk(j + 1, 0))
                step(Blk(j + 1, 0), Blk(j + 1, 1))
            step(Blk(BLOCKS // 2 - 1, 1), None)
            sp.wait_ge(made, FILL_MADE)
            for e in range(EXPERTS):
                r = sp.value_load(fill_t[0:1, e:e + 1], min_val=e * REGION, max_val=e * REGION + TOKENS)
                sp.dma_start(rows_sorted[bass.ds(r, P), :], blank[:, :]).then_inc(filled, 16)
            sp.wait_ge(filled, 16 * (EXPERTS + 1))
            sp.wait_ge(tail_out, 16)
            for b in range(BATCHES):
                sp.wait_ge(x2_out[b], 16 * BLOCKS // 2)

        @block.gpsimd
        def _(pool):
            for t, v in ((ident, 0.0), (ident_bf, 0.0), (ones_bf, 1.0), (before, 1.0), (minus_head, 0.0),
                         (minus_half, -0.5), (eps, EPS), (spare_pool, 0.0), (spare_dve, 0.0), (exp_bias, float(np.log(PROB_SCALE))), (mx_t, 0.0), (earlier, 0.0), (rows, 0.0),
                         *((k, 0.0) for k in k_hi + k_lo)):
                pool.memset(t[:].bitcast(F32) if t in k_hi + k_lo else t[:], v).then_inc(const_set, 1)
            pool.iota(iota_i[:, :, :], pattern=[[0, SUB], [1, EXPERTS]], base=0, channel_multiplier=0).then_inc(const_set, 1)
            for b in range(BATCHES):
                pool.iota(tok_i[b][:, :], pattern=[[P, SUB]], base=b * SEQ, channel_multiplier=1).then_inc(const_set, 1)
            pool.memset(counts[:, :], 0.0).then_inc(const_set, 1)
            pool.memset(mx[:], 0.0).then_inc(const_set, 1)
            pool.wait_ge(const_set, CONST_SET)
            for t in (ident, ident_bf):
                pool.affine_select(out=t[:, :], in_=t[:, :], compare_op=ALU.not_equal, fill=1.0, base=0,
                                   pattern=[[-1, P]], channel_multiplier=1).then_inc(const_cut, 1)
            pool.affine_select(out=before[:, :], in_=before[:, :], compare_op=ALU.is_gt, fill=0.0, base=0,
                               pattern=[[1, P]], channel_multiplier=-1).then_inc(const_cut, 1)
            for part in range(2):
                if part:
                    pool.wait_ge(const_cut, 4)
                pool.affine_select(out=minus_head[:, :, :], in_=minus_head[:, :, :], compare_op=ALU.not_equal, fill=-1.0,
                                   base=-part * HEADS, pattern=[[-1, HEADS], [0, KEYS]],
                                   channel_multiplier=1).then_inc(const_cut, 1)

            pool.memset(blank[:, :], 0.0).then_inc(sched_set, 1)
            pool.memset(ones8[:, :], 1.0).then_inc(sched_set, 1)
            pool.memset(sign[:, :], 1.0).then_inc(sched_set, 1)
            pool.iota(slot_i[:, :], pattern=[[1, SLOTS]], base=0, channel_multiplier=0).then_inc(sched_set, 1)
            pool.iota(steps_i[:, :, :], pattern=[[0, EXPERTS], [P, MOST]], base=0, channel_multiplier=0).then_inc(sched_set, 1)
            pool.iota(eight_i[:, :], pattern=[[REGION, EXPERTS]], base=0, channel_multiplier=0).then_inc(sched_set, 1)
            pool.wait_ge(sched_set, 6)
            pool.iota(blank[:, TOKEN:TOKEN + 1].bitcast(I32), pattern=[[0, 1]], base=TOKENS, channel_multiplier=1).then_inc(sched_set, 1)
            pool.memset(sign[:, 1::2], -1.0).then_inc(sched_set, 1)

            def rstd(n, mv, var, rs, mv_done, var_done, rstd_done):
                pool.wait_ge(mv_done, n * SUB + SUB)
                pool.tensor_tensor(var[:, :], mv[:, :, 1], eps[:, :], ALU.add).then_inc(var_done, 1)
                pool.wait_ge(var_done, n + 1)
                pool.tensor_tensor(rs[:, :], var[:, :], minus_half[:, :], ALU.pow).then_inc(rstd_done, 1)

            def rstd_first(nxt):
                rstd(nxt.n, mv1, var1, rstd1, mv1_done, var1_done, rstd1_done)

            def rstd_second(cur):
                rstd(cur.n, mv2, var2, rstd2, mv2_done, var2_done, rstd2_done)

            def out_lo(cur, c):
                pool.wait_ge(o_hi_done, cur.n * DC + c + 1)
                pool.tensor_tensor(o_lo[:, c, :], o_f[:, c % 2, :], o_hi[:, c, :].bitcast(F32), ALU.subtract).then_inc(o_lo_done, 1)

            def add_bias(nxt, s):
                if s == 0:
                    pool.wait_ge(xn_done, nxt.n + 1)
                    if nxt.first:
                        pool.wait_ge(gated, 2)
                pool.tensor_tensor(x[nxt.b][:, s, :], x[nxt.b][:, s, :], bo_row[:, :], ALU.add).then_inc(xb_done, 1)

            def prob_lo(cur, h):
                pool.wait_ge(exp_done, cur.n * HEADS + h + 1)
                pool.tensor_tensor(p_lo[:, h % HELD, :], prob[:, h % HELD_F, :], p_hi[:, h % HELD, :],
                                   ALU.subtract).then_inc(p_lo_odd, 1)

            def scatter(prv):
                pool.wait_ge(place_step, prv.n * 5 + 5)
                pool.wait_ge(meta_done, prv.n * 6 + 6)
                hold(pool, spare_pool, held_pool, prv.n)
                for k in range(TOPK):
                    for s in range(SUB):
                        pool.indirect_dma_start(
                            out=rows_sorted, out_offset=bass.IndirectOffsetOnAxis(ap=target[:, k, s:s + 1].bitcast(U32), axis=0),
                            in_=rows[:, s, :], in_offset=None, bounds_check=SORTED_ROWS - 1, oob_is_err=True).then_inc(scattered, 16)

            def step(cur, nxt, prv):
                for h in range(1, HEADS, 2):
                    prob_lo(cur, h)
                    if nxt and h == 5:
                        rstd_first(nxt)
                    if h == 13:
                        out_lo(cur, 0)
                    if h == 15:
                        out_lo(cur, 1)
                    if nxt and h >= 9:
                        add_bias(nxt, (h - 9) // 2)
                out_lo(cur, 2)
                out_lo(cur, 3)
                if prv:
                    scatter(prv)
                rstd_second(cur)

            rstd_first(Blk(0, 0))
            for s in range(SUB):
                add_bias(Blk(0, 0), s)
            step(Blk(0, 0), Blk(0, 1), None)
            with pool.Fori(0, BLOCKS // 2 - 1, 1) as j:
                step(Blk(j, 1), Blk(j + 1, 0), Blk(j, 0))
                step(Blk(j + 1, 0), Blk(j + 1, 1), Blk(j, 1))
            pool.wait_ge(q_hi_done, BLOCKS * DC)
            stage(pool, A, S, 0)
            step(Blk(BLOCKS // 2 - 1, 1), None, Blk(BLOCKS // 2 - 1, 0))
            scatter(Blk(BLOCKS // 2 - 1, 1))
            pool.wait_ge(scattered, 16 * TOPK * SUB * BLOCKS)

        @block.scalar
        def _(act):
            act.wait_ge(small_in, 16 * SMALL)
            act.activation(tanh_g[:, :], gates[:, :], ACT.Tanh).then_inc(tanh_done, 1)
            act.wait_ge(wq_in, 16)
            act.activation(wq_hi[:, :, :], wq_raw[:, :, :], ACT.Copy).then_inc(w_hi_done, 1)
            act.wait_ge(gated, 2)
            act.activation(wo_hi[:, :, :], wo_raw[:, :, :], ACT.Copy).then_inc(w_hi_done, 1)
            def ctx_halves(b):
                act.wait_ge(ctx_t, b + 1)
                wait(act, kv_full, b)
                act.activation(o_hi[:, 0, :], ps_max[:, :], ACT.Copy).then_inc(ctx_hi, 1)

            def keys_hi(b):
                act.wait_ge(kt_full, b + 1)
                if b == 0:
                    act.wait_ge(const_set, CONST_SET)
                for i in range(PER_CHUNK):
                    r = slice(DK * i, DK * i + DK)
                    last = act.activation(k_hi[b][r, :, i, :], psL[r, :].rearrange("p (c k) -> p c k", c=DC), ACT.Copy)
                last.then_inc(kt_hi, 1)

            def halves(nxt, c):
                act.wait_ge(f_full, nxt.f_transposes(c) + 1)
                act.activation(xt_hi[:, c, :], psF[c % 2][:, :], ACT.Copy).then_inc(xt_hi_done, 1)

            def queries(nxt, m):
                act.wait_ge(f_full, nxt.f_queries(m) + 1)
                act.activation(q_hi[:, m, :], psF[m % 2][:, :], ACT.Identity, bias=bq_col[:, m:m + 1]).then_inc(q_hi_done, 1)

            def exps(cur, h):
                act.wait_ge(b_full, cur.n * HEADS + h + 1)
                wait(act, pv_done, cur.slot_free(h))
                act.activation(p_hi[:, h % HELD, :], psB[h % 2][:, :], ACT.Exp, bias=exp_bias[:, 0:1],
                               scale=float(DK) ** -0.5)
                if h >= HELD_F:
                    act.wait_ge(p_lo_even if h % 2 else p_lo_odd, cur.low(h - HELD_F))
                act.activation(prob[:, h % HELD_F, :], psB[h % 2][:, :], ACT.Exp, bias=exp_bias[:, 0:1],
                               scale=float(DK) ** -0.5).then_inc(exp_done, 1)

            def copy_sums(cur, c):
                act.wait_ge(pv_done, cur.n * HEADS + PER_CHUNK * c + PER_CHUNK)
                wait(act, inv_t_full, cur.n * DC + c)
                act.activation(sums[:, :], psD[:, :], ACT.Copy)
                wait(act, o_done, cur.n * DC + c)
                act.activation(o_raw[:, :], psO[:, :], ACT.Copy).then_inc(copied, 1)

            def out_hi(cur, c):
                act.wait_ge(o_done, cur.n * DC + c + 1)
                if c == 0 and not cur.first:
                    act.wait_ge(f_full, cur.n * 16 + 4)
                act.activation(o_hi[:, c, :], o_f[:, c % 2, :], ACT.Copy).then_inc(o_hi_done, 1)

            def routing_hi(prv, s):
                act.wait_ge(f_full, prv.f_routing(s) + 1)
                act.activation(r_hi[:, s, :], psF[s % 2][:, :], ACT.Copy, scale=X_SCALE).then_inc(r_hi_done, 1)

            def weight_exp(prv):
                act.wait_ge(route_step, prv.n * LINKS + LINKS)
                act.activation(wexp[:, :], wdiff[:, :], ACT.Exp).then_inc(wexp_done, 1)

            def step(cur, nxt, prv):
                for h in range(HEADS):
                    exps(cur, h)
                    if prv and h in ROUTING_T:
                        routing_hi(prv, ROUTING_T[h])
                    if nxt and h in TRANSPOSES:
                        halves(nxt, TRANSPOSES[h])
                    if nxt and h in QUERIES:
                        queries(nxt, QUERIES[h])
                    if h in (7, 11, 15):
                        copy_sums(cur, (h - LAG) // PER_CHUNK)
                    if h in (11, 15):
                        out_hi(cur, (h - 11) // PER_CHUNK)
                    if prv and h == 13:
                        weight_exp(prv)
                if nxt:
                    queries(nxt, 1)
                    queries(nxt, 2)
                copy_sums(cur, 3)
                out_hi(cur, 2)
                if nxt:
                    queries(nxt, 3)
                out_hi(cur, 3)

            ctx_halves(0)
            keys_hi(0)
            ctx_halves(1)
            for c in range(DC):
                halves(Blk(0, 0), c)
            keys_hi(1)
            for m in range(DC):
                queries(Blk(0, 0), m)
            step(Blk(0, 0), Blk(0, 1), None)
            with act.Fori(0, BLOCKS // 2 - 1, 1) as j:
                step(Blk(j, 1), Blk(j + 1, 0), Blk(j, 0))
                step(Blk(j + 1, 0), Blk(j + 1, 1), Blk(j, 1))
            step(Blk(BLOCKS // 2 - 1, 1), None, Blk(BLOCKS // 2 - 1, 0))
            for s in range(SUB):
                routing_hi(Blk(BLOCKS // 2 - 1, 1), s)
            weight_exp(Blk(BLOCKS // 2 - 1, 1))

        @block.tensor
        def _(pe):
            def split3(dst, hi, lo, w_hi, w_lo, chunks=range(DC)):
                for c in chunks:
                    pe.matmul(dst, hi(c), w_hi[:, c, :], start=c == 0, stop=False)
                    pe.matmul(dst, hi(c), w_lo[:, c, :], start=False, stop=False)
                    last = pe.matmul(dst, lo(c), w_hi[:, c, :], start=False, stop=c == DC - 1)
                return last

            pe.wait_ge(const_cut, CONST_CUT)
            pe.wait_ge(ctx_in, 16)
            def keys(b):
                wait(pe, ctx_lo, b)
                for c in range(DC):
                    last = pe.transpose(ps_max[:, c * P:c * P + P], ctx_raw[:, b, c * P:c * P + P], ident[:, :])
                last.then_inc(ctx_t, 1)
                pe.wait_ge(ctx_lo, b + 1)
                pe.wait_ge(w_lo_done, 1)
                wait(pe, kv_done, b)
                split3(psB[0][:, :], lambda c: o_hi[:, 0, c * P:c * P + P], lambda c: o_lo[:, 0, c * P:c * P + P],
                       wq_hi, wq_lo).then_inc(kv_full, 1)

            def keys_t(b):
                pe.wait_ge(kv_done, b + 1)
                wait(pe, kt_lo, b)
                for c in range(DC):
                    last = pe.transpose(psL[:, c * P:c * P + P], kv[:, c * P:c * P + P], ident[:, :])
                last.then_inc(kt_full, 1)

            def transposes(nxt, c):
                pe.wait_ge(xn_done, nxt.n + 1)
                wait(pe, f_free, nxt.f_transposes(c) - 1)
                for s in range(SUB):
                    last = pe.transpose(psF[c % 2][:, s * P:s * P + P], xn[:, s, c * P:c * P + P], ident[:, :])
                last.then_inc(f_full, 1)

            def queries(nxt, m, chunks=range(DC)):
                if 0 in chunks:
                    pe.wait_ge(f_free, nxt.f_transposes(3) + 1)
                    pe.wait_ge(f_free, nxt.f_queries(m) - 1)
                for c in chunks:
                    ms = slice(m * P, m * P + P)
                    pe.matmul(psF[m % 2][:, :], wq_hi[:, c, ms], xt_hi[:, c, :], start=c == 0, stop=False)
                    pe.matmul(psF[m % 2][:, :], wq_hi[:, c, ms], xt_lo[:, c, :], start=False, stop=False)
                    last = pe.matmul(psF[m % 2][:, :], wq_lo[:, c, ms], xt_hi[:, c, :], start=False, stop=c == DC - 1)
                if DC - 1 in chunks:
                    last.then_inc(f_full, 1)

            def maxima(nxt, pair):
                for u in (2 * pair, 2 * pair + 1):
                    c, s = u // SUB, u % SUB
                    if s == 0:
                        pe.wait_ge(q_hi_done, nxt.n * DC + c + 1)
                    if u == 0:
                        wait(pe, exp_done, nxt.n * HEADS)
                    if u >= 2:
                        pe.wait_ge(m_free, nxt.n * 16 + u - 1)
                    pe.matmul(psB[u % 2][:, :], q_hi[:, c, s * P:s * P + P],
                              k_hi[nxt.b][:, c, :, :].rearrange("p i k -> p (i k)"), start=True, stop=True).then_inc(m_full, 1)

            def maxima_t(nxt):
                pe.wait_ge(mx_step, nxt.n * 3 + 3)
                for s in range(SUB):
                    last = pe.transpose(psM[0:2 * HEADS, s * P:s * P + P], mx_parts[:, s, :], ident_bf[:, :])
                last.then_inc(mx_full, 1)

            def scores(cur, h):
                n, c, i = cur.n * HEADS + h, h // PER_CHUNK, h % PER_CHUNK
                if h == 0:
                    pe.wait_ge(mx_t_done, cur.n + 1)
                wait(pe, exp_done, n - 1)
                dst = psB[h % 2][:, :]
                pe.matmul(dst, k_hi[cur.b][:, c, i, :], q_hi[:, c, :], start=True, stop=False)
                pe.matmul(dst, k_hi[cur.b][:, c, i, :], q_lo[:, c, :], start=False, stop=False)
                pe.matmul(dst, k_lo[cur.b][:, c, i, :], q_hi[:, c, :], start=False, stop=False)
                pe.matmul(dst, minus_head[:, h, :], mx_t[:, :], start=False, stop=True).then_inc(b_full, 1)

            def values(cur, h):
                n, c, i = cur.n * HEADS + h, h // PER_CHUNK, h % PER_CHUNK
                pe.wait_ge(p_lo_odd if h % 2 else p_lo_even, cur.low(h))
                if i == 0:
                    wait(pe, copied, cur.n * DC + c)
                r = slice(DK * i, DK * i + DK)
                hi, lo = p_hi[:, h % HELD, :], p_lo[:, h % HELD, :]
                v = [v_parts[cur.b][:, k, h * DK:h * DK + DK] for k in range(3)]
                for k, (part, p) in enumerate(((v[0], hi), (v[1], hi), (v[2], hi), (v[0], lo), (v[1], lo))):
                    pe.matmul(psO[r, :], part, p, start=k == 0, stop=k == 4)
                pe.matmul(psD[r, :], ones_bf[:, 0:DK], hi, start=True, stop=False)
                pe.matmul(psD[r, :], ones_bf[:, 0:DK], lo, start=False, stop=True).then_inc(pv_done, 1)

            def sums_t(cur, c):
                pe.wait_ge(copied, cur.n * DC + c + 1)
                wait(pe, o_done, cur.n * DC + c)
                for s in range(SUB):
                    last = pe.transpose(ps_max[:, s * P:s * P + P], sums[:, s * P:s * P + P], ident[:, :])
                last.then_inc(sums_t_full, 1)

            def inverses_t(cur, c):
                pe.wait_ge(inv_done, (cur.n * DC + c) * 2 + 2)
                for s in range(SUB):
                    last = pe.transpose(ps_max[:, s * P:s * P + P], sums[:, s * P:s * P + P], ident[:, :])
                last.then_inc(inv_t_full, 1)

            def output(cur, s, chunks=range(DC)):
                if 0 in chunks:
                    pe.wait_ge(o_lo_done, cur.n * DC + DC)
                    pe.wait_ge(f_free, cur.f_output(s) - 1)
                ss = slice(s * P, s * P + P)
                last = split3(psF[s % 2][:, :], lambda c: o_hi[:, c, ss], lambda c: o_lo[:, c, ss], wo_hi, wo_lo, chunks)
                if DC - 1 in chunks:
                    last.then_inc(f_full, 1)

            def routing_t(prv, s):
                pe.wait_ge(xn2_done, prv.n + 1)
                pe.wait_ge(f_free, prv.f_routing(s) - 1)
                for c in range(DC):
                    last = pe.transpose(psF[s % 2][:, c * P:c * P + P], rows[:, s, c * P:c * P + P], ident[:, :])
                last.then_inc(f_full, 1)

            def routing_logits(prv):
                pe.wait_ge(f_free, prv.f_routing(3) + 1)
                wait(pe, place_step, prv.n * 5)
                for s in range(SUB):
                    for c in range(DC):
                        for k, half in enumerate((r_hi, r_lo)):
                            last = pe.matmul(LG[:, s, 0:3 * EXPERTS], half[:, s, c * P:c * P + P],
                                             wr_parts[:, c, :, :].rearrange("p k e -> p (k e)"),
                                             start=c == 0 and k == 0, stop=c == DC - 1 and k == 1)
                last.then_inc(lg_full, 1)

            def ranks(prv):
                pe.wait_ge(route_step, prv.n * LINKS + LINKS)
                dst = RK[:, :, :].rearrange("p s e -> p (s e)")
                pe.matmul(dst, before[:, :], chosen_any[:, :, :].rearrange("p s e -> p (s e)"), start=True, stop=False)
                pe.matmul(dst, ones_bf[:, :], earlier[:, 0:SUB, :].rearrange("p s e -> p (s e)"),
                          start=False, stop=True).then_inc(rk_full, 1)

            def step(cur, nxt, prv):
                for h in range(HEADS):
                    scores(cur, h)
                    if h >= LAG and h % PER_CHUNK:
                        values(cur, h - LAG)
                    if h in SUMS_T:
                        sums_t(cur, SUMS_T[h])
                    if h in INVERSES_T:
                        inverses_t(cur, INVERSES_T[h])
                    if prv and h in ROUTING_T:
                        routing_t(prv, ROUTING_T[h])
                    if prv and h == 9:
                        routing_logits(prv)
                    if nxt and h in TRANSPOSES:
                        transposes(nxt, TRANSPOSES[h])
                    if prv and h == 14:
                        ranks(prv)
                    if h >= LAG and h % PER_CHUNK == 0:
                        values(cur, h - LAG)
                    if nxt and h in QUERIES:
                        queries(nxt, QUERIES[h])
                if nxt:
                    queries(nxt, 1)
                values(cur, HEADS - 4)
                sums_t(cur, 2)
                for h in range(HEADS - 3, HEADS):
                    values(cur, h)
                if nxt:
                    queries(nxt, 2)
                inverses_t(cur, 2)
                if not nxt:
                    sums_t(cur, 3)
                    inverses_t(cur, 3)
                    for s in range(SUB):
                        output(cur, s)
                    return
                maxima(nxt, 0)
                queries(nxt, 3, (0, 1))
                maxima(nxt, 1)
                queries(nxt, 3, (2, 3))
                sums_t(cur, 3)
                maxima(nxt, 2)
                inverses_t(cur, 3)
                maxima(nxt, 3)
                maxima(nxt, 4)
                output(cur, 0, (0, 1))
                maxima(nxt, 5)
                output(cur, 0, (2, 3))
                maxima(nxt, 6)
                output(cur, 1, (0, 1))
                maxima(nxt, 7)
                output(cur, 1, (2, 3))
                output(cur, 2)
                maxima_t(nxt)
                output(cur, 3)

            keys(0)
            keys_t(0)
            keys(1)
            for c in range(DC):
                transposes(Blk(0, 0), c)
            keys_t(1)
            for m in range(DC):
                queries(Blk(0, 0), m)
            pe.wait_ge(kt_lo, BATCHES)
            pe.wait_ge(v_done, BATCHES * 5)
            pe.wait_ge(w_lo_done, 2)
            pe.wait_ge(wr_done, 5)
            for pair in range(PAIRS):
                maxima(Blk(0, 0), pair)
            maxima_t(Blk(0, 0))
            step(Blk(0, 0), Blk(0, 1), None)
            with pe.Fori(0, BLOCKS // 2 - 1, 1) as j:
                step(Blk(j, 1), Blk(j + 1, 0), Blk(j, 0))
                step(Blk(j + 1, 0), Blk(j + 1, 1), Blk(j, 1))
            final = Blk(BLOCKS // 2 - 1, 1)
            step(final, None, Blk(BLOCKS // 2 - 1, 0))
            for s in range(SUB):
                routing_t(final, s)
            routing_logits(final)
            ranks(final)
            pe.wait_ge(place_step, BLOCKS * 5)
            pe.matmul(TOTAL, ones_bf[:, :], earlier[:, SUB, :], start=True, stop=True).then_inc(total_full, 1)

        @block.vector
        def _(dve):
            dve.wait_ge(const_set, CONST_SET)
            dve.tensor_copy(iota_f[:, :, :], iota_i[:, :, :]).then_inc(const_f, 1)
            for b in range(BATCHES):
                dve.tensor_copy(tok_f[b][:, :], tok_i[b][:, :]).then_inc(const_f, 1)
            dve.wait_ge(const_f, 1)
            dve.tensor_scalar(region_f[:, :, :], iota_f[:, :, :], float(REGION), None, ALU.mult).then_inc(const_f, 1)
            dve.wait_ge(small_in, 16 * SMALL)
            dve.wait_ge(tanh_done, 1)
            dve.tensor_scalar(bo_row[:, :], bo_row[:, :], tanh_g[:, 0:1], None, ALU.mult).then_inc(gated, 1)
            dve.wait_ge(wo_in, 16)
            dve.tensor_scalar(wo_raw[:, :, :], wo_raw[:, :, :], tanh_g[:, 0:1], None, ALU.mult).then_inc(gated, 1)
            dve.wait_ge(w_hi_done, 1)
            dve.tensor_tensor(wq_lo[:, :, :], wq_raw[:, :, :], wq_hi[:, :, :].bitcast(F32), ALU.subtract).then_inc(w_lo_done, 1)
            dve.wait_ge(w_hi_done, 2)
            dve.tensor_tensor(wo_lo[:, :, :], wo_raw[:, :, :], wo_hi[:, :, :].bitcast(F32), ALU.subtract).then_inc(w_lo_done, 1)
            dve.tensor_copy(wr_parts[:, :, 0, :], wr[:, :, :]).then_inc(wr_done, 1)
            dve.wait_ge(wr_done, 1)
            dve.tensor_tensor(wr_rest[:, 0, :, :], wr[:, :, :], wr_parts[:, :, 0, :], ALU.subtract).then_inc(wr_done, 1)
            dve.wait_ge(wr_done, 2)
            dve.tensor_copy(wr_parts[:, :, 1, :], wr_rest[:, 0, :, :]).then_inc(wr_done, 1)
            dve.wait_ge(wr_done, 3)
            dve.tensor_tensor(wr_rest[:, 1, :, :], wr_rest[:, 0, :, :], wr_parts[:, :, 1, :], ALU.subtract).then_inc(wr_done, 1)
            dve.wait_ge(wr_done, 4)
            dve.tensor_copy(wr_parts[:, :, 2, :], wr_rest[:, 1, :, :]).then_inc(wr_done, 1)
            def ctx_halves(b):
                dve.wait_ge(ctx_hi, b + 1)
                dve.tensor_tensor(o_lo[:, 0, :], ps_max[:, :], o_hi[:, 0, :].bitcast(F32), ALU.subtract).then_inc(ctx_lo, 1)

            def keys(b):
                dve.wait_ge(kv_full, b + 1)
                wait(dve, kt_full, b)
                dve.tensor_tensor(kv[:, :], psB[0][:, :], bq_row[:, :], ALU.add).then_inc(kv_done, 1)

            def values_and_keys_lo(b):
                dve.wait_ge(kv_done, b + 1)
                dve.tensor_copy(v_parts[b][:, 0, :], kv[:, :]).then_inc(v_done, 1)
                dve.wait_ge(v_done, b * 5 + 1)
                dve.tensor_tensor(prob[:, 0, :], kv[:, :], v_parts[b][:, 0, :], ALU.subtract).then_inc(v_done, 1)
                dve.wait_ge(v_done, b * 5 + 2)
                dve.tensor_copy(v_parts[b][:, 1, :], prob[:, 0, :]).then_inc(v_done, 1)
                dve.wait_ge(v_done, b * 5 + 3)
                dve.tensor_tensor(prob[:, 1, :], prob[:, 0, :], v_parts[b][:, 1, :], ALU.subtract).then_inc(v_done, 1)
                dve.wait_ge(v_done, b * 5 + 4)
                dve.tensor_copy(v_parts[b][:, 2, :], prob[:, 1, :]).then_inc(v_done, 1)
                dve.wait_ge(kt_hi, b + 1)
                for i in range(PER_CHUNK):
                    r = slice(DK * i, DK * i + DK)
                    last = dve.tensor_tensor(k_lo[b][r, :, i, :], psL[r, :].rearrange("p (c k) -> p c k", c=DC),
                                             k_hi[b][r, :, i, :].bitcast(F32), ALU.subtract)
                last.then_inc(kt_lo, 1)

            def ln_stats(n, src, stats, mv, stats_done, mv_done, held):
                for s in range(SUB):
                    dve.bn_stats(stats[:, s, :], src[:, s, :]).then_inc(stats_done, 1)
                dve.wait_ge(stats_done, n * SUB + SUB)
                hold(dve, spare_dve, held_dve, held)
                for s in range(SUB):
                    dve.bn_aggr(mv[:, s, :], stats[:, s, :]).then_inc(mv_done, 1)

            def ln1_stats(nxt):
                dve.wait_ge(x_in[nxt.b], 16 * nxt.q + 16)
                ln_stats(nxt.n, x[nxt.b], stats1, mv1, stats1_done, mv1_done,
                         2 * nxt.n - (0 if nxt.first else 1))

            def ln1(nxt):
                dve.wait_ge(rstd1_done, nxt.n + 1)
                for s in range(SUB):
                    last = dve.tensor_scalar(xn[:, s, :], x[nxt.b][:, s, :], mv1[:, s, 0:1], rstd1[:, s:s + 1], ALU.subtract, ALU.mult)
                last.then_inc(xn_done, 1)

            def ln2_stats(cur):
                dve.wait_ge(f_free, cur.f_output(3) + 1)
                ln_stats(cur.n, x[cur.b], stats2, mv2, stats2_done, mv2_done,
                         2 * cur.n + (1 if cur.last else 2))

            def ln2(prv):
                dve.wait_ge(rstd2_done, prv.n + 1)
                wait(dve, scattered, prv.n * (16 * TOPK * SUB))
                for s in range(SUB):
                    last = dve.tensor_scalar(rows[:, s, 0:D], x[prv.b][:, s, :], mv2[:, s, 0:1], rstd2[:, s:s + 1], ALU.subtract, ALU.mult)
                last.then_inc(xn2_done, 1)

            def halves(nxt, c):
                dve.wait_ge(xt_hi_done, nxt.n * DC + c + 1)
                dve.tensor_tensor(xt_lo[:, c, :], psF[c % 2][:, :], xt_hi[:, c, :].bitcast(F32), ALU.subtract).then_inc(f_free, 1)

            def queries(nxt, m):
                dve.wait_ge(q_hi_done, nxt.n * DC + m + 1)
                dve.scalar_tensor_tensor(out=q_lo[:, m, :], in0=psF[m % 2][:, :], scalar=bq_col[:, m:m + 1],
                                         in1=q_hi[:, m, :].bitcast(F32), op0=ALU.add, op1=ALU.subtract).then_inc(f_free, 1)

            def maxima(nxt, pair):
                for u in (2 * pair, 2 * pair + 1):
                    c, s = u // SUB, u % SUB
                    dve.wait_ge(m_full, nxt.n * 16 + u + 1)
                    dve.tensor_reduce(mx[:, s, PER_CHUNK * c:PER_CHUNK * c + PER_CHUNK],
                                      psB[u % 2][:, :].rearrange("p (i k) -> p i k", i=PER_CHUNK), AX_X, ALU.max).then_inc(m_free, 1)

            def maxima_parts(nxt):
                dve.wait_ge(m_free, nxt.n * 16 + 16)
                dve.tensor_copy(mx_parts[:, :, 0:HEADS], mx[:, :, :]).then_inc(mx_step, 1)
                dve.wait_ge(mx_step, nxt.n * 3 + 1)
                dve.tensor_tensor(mx_rest[:, :, :], mx[:, :, :], mx_parts[:, :, 0:HEADS], ALU.subtract).then_inc(mx_step, 1)
                dve.wait_ge(mx_step, nxt.n * 3 + 2)
                dve.tensor_copy(mx_parts[:, :, HEADS:], mx_rest[:, :, :]).then_inc(mx_step, 1)

            def maxima_t(nxt):
                dve.wait_ge(mx_full, nxt.n + 1)
                dve.tensor_copy(mx_t[0:2 * HEADS, :], psM[0:2 * HEADS, 0:BLOCK]).then_inc(mx_t_done, 1)

            def prob_lo(cur, h):
                dve.wait_ge(exp_done, cur.n * HEADS + h + 1)
                dve.tensor_tensor(p_lo[:, h % HELD, :], prob[:, h % HELD_F, :], p_hi[:, h % HELD, :],
                                  ALU.subtract).then_inc(p_lo_even, 1)

            def invert(cur, c):
                dve.wait_ge(sums_t_full, cur.n * DC + c + 1)
                dve.reciprocal(inverses[:, :, :], ps_max[:, :].rearrange("p (s r) -> p s r", s=SUB)[:, :, ::DK]).then_inc(inv_done, 1)
                dve.wait_ge(inv_done, (cur.n * DC + c) * 2 + 1)
                dve.tensor_copy(sums[:, :].rearrange("p (s i k) -> p s i k", s=SUB, k=DK),
                                inverses[:, :, :].unsqueeze(3).to_broadcast([P, SUB, PER_CHUNK, DK])).then_inc(inv_done, 1)

            def divide(cur, c):
                dve.wait_ge(inv_t_full, cur.n * DC + c + 1)
                wait(dve, o_lo_done, cur.n * DC + c - 1)
                dve.tensor_tensor(o_f[:, c % 2, :], ps_max[:, :], o_raw[:, :], ALU.mult).then_inc(o_done, 1)

            def output(cur, s):
                dve.wait_ge(xb_done, cur.n * SUB + SUB)
                dve.wait_ge(f_full, cur.f_output(s) + 1)
                dve.tensor_tensor(x[cur.b][:, s, :], psF[s % 2][:, :], x[cur.b][:, s, :], ALU.add).then_inc(f_free, 1)

            def routing_lo(prv, s):
                dve.wait_ge(r_hi_done, prv.n * SUB + s + 1)
                dve.scalar_tensor_tensor(out=r_lo[:, s, :], in0=psF[s % 2][:, :], scalar=X_SCALE, in1=r_hi[:, s, :],
                                         op0=ALU.mult, op1=ALU.subtract).then_inc(f_free, 1)

            def route(prv, part):
                base = prv.n * LINKS
                done = [{0: 0, 1: 4, 2: 13}[part]]

                def link(ins):
                    done[0] += 1
                    ins.then_inc(route_step, 1)

                def after(k):
                    dve.wait_ge(route_step, base + k)

                if part == 0:
                    dve.wait_ge(lg_full, prv.n + 1)
                    link(dve.tensor_reduce(lsum[:, :, :], LG[:, :, 0:3 * EXPERTS].rearrange("p s (k e) -> p s e k", k=3), AX_X, ALU.add))
                    after(1)
                    link(dve.tensor_scalar(logits[:, :, :], lsum[:, :, :], 1.0 / X_SCALE, None, ALU.mult))
                    after(2)
                    link(dve.tensor_tensor(logits[:, :, :], logits[:, :, :], rb_row[:, :].unsqueeze(1).to_broadcast([P, SUB, EXPERTS]), ALU.add))
                    after(3)
                    link(dve.tensor_copy(earlier[:, 0, :], earlier[:, SUB, :]))
                if part == 1:
                    for s in range(SUB):
                        link(dve.max(top[:, s, :], logits[:, s, :]))
                    after(8)
                    link(dve.tensor_tensor(wdiff[:, :], top[:, :, 1], top[:, :, 0], ALU.subtract))
                    for s in range(SUB):
                        link(dve.max_index(top_ix[:, s, :], top[:, s, :], logits[:, s, :]))
                if part == 2:
                    after(13)
                    link(dve.tensor_copy(pick[:, :, :], top_ix[:, :, 0:TOPK]))
                    after(14)
                    for k in range(TOPK):
                        link(dve.tensor_tensor(chosen[k][:, :, :], iota_f[:, :, :],
                                               pick[:, :, k:k + 1].to_broadcast([P, SUB, EXPERTS]), ALU.is_equal))
                    after(16)
                    link(dve.tensor_tensor(chosen_any[:, :, :], chosen[0][:, :, :], chosen[1][:, :, :], ALU.add))
                    for s in range(SUB):
                        after(17 + s)
                        link(dve.tensor_tensor(earlier[:, s + 1, :], earlier[:, s, :], chosen_any[:, s, :], ALU.add))
                    assert done[0] == LINKS

            def weights(prv):
                base = prv.n * 6
                dve.wait_ge(wexp_done, prv.n + 1)
                dve.tensor_scalar(wden[:, :], wexp[:, :], 1.0, None, ALU.add).then_inc(meta_done, 1)
                dve.wait_ge(meta_done, base + 1)
                dve.reciprocal(wrec[:, :], wden[:, :]).then_inc(meta_done, 1)
                dve.wait_ge(meta_done, base + 2)
                dve.tensor_scalar(whigh[:, :], wrec[:, :], tanh_g[:, 1:2], None, ALU.mult).then_inc(meta_done, 1)
                dve.wait_ge(meta_done, base + 3)
                dve.tensor_tensor(rows[:, :, W_LOW], whigh[:, :], wexp[:, :], ALU.mult).then_inc(meta_done, 1)
                dve.wait_ge(meta_done, base + 4)
                dve.tensor_tensor(rows[:, :, W_DIFF], whigh[:, :], rows[:, :, W_LOW], ALU.subtract).then_inc(meta_done, 1)
                dve.tensor_copy(rows[:, :, FIRST_EXPERT], pick[:, :, 0])
                dve.tensor_copy(rows[:, :, TOKEN].bitcast(I32), tok_f[prv.b][:, :]).then_inc(meta_done, 1)
                dve.wait_ge(meta_done, base + 6)
                dve.tensor_scalar(tok_f[prv.b][:, :], tok_f[prv.b][:, :], float(BLOCK), None, ALU.add).then_inc(const_f, 1)

            def targets(prv):
                base = prv.n * 5
                dve.wait_ge(rk_full, prv.n + 1)
                dve.tensor_tensor(place[:, :, :], RK[:, :, :], region_f[:, :, :], ALU.add).then_inc(place_step, 1)
                dve.wait_ge(place_step, base + 1)
                for k in range(TOPK):
                    dve.tensor_tensor(place_k[:, k, :, :], place[:, :, :], chosen[k][:, :, :], ALU.mult).then_inc(place_step, 1)
                dve.wait_ge(place_step, base + 3)
                dve.tensor_reduce(place_s[:, :, :], place_k[:, :, :, :], AX_X, ALU.add).then_inc(place_step, 1)
                dve.wait_ge(place_step, base + 4)
                dve.tensor_copy(target[:, :, :], place_s[:, :, :]).then_inc(place_step, 1)

            def step(cur, nxt, prv):
                for h in range(HEADS):
                    if h % 2 == 0:
                        prob_lo(cur, h)
                    if prv and h == 1:
                        ln2(prv)
                    if prv and h in ROUTING_T:
                        routing_lo(prv, ROUTING_T[h])
                    if nxt and h == 7:
                        ln1_stats(nxt)
                    if nxt and h == 9:
                        ln1(nxt)
                    if nxt and h in TRANSPOSES:
                        halves(nxt, TRANSPOSES[h])
                    if prv and h in ROUTE:
                        route(prv, ROUTE[h])
                    if nxt and h in QUERIES:
                        queries(nxt, QUERIES[h])
                    if prv and h == 14:
                        weights(prv)
                    if prv and h == 15:
                        targets(prv)
                    if h in SUMS_T:
                        invert(cur, SUMS_T[h])
                    if h in INVERSES_T:
                        divide(cur, INVERSES_T[h])
                if nxt:
                    queries(nxt, 1)
                invert(cur, 2)
                if nxt:
                    queries(nxt, 2)
                divide(cur, 2)
                if nxt:
                    maxima(nxt, 0)
                    maxima(nxt, 1)
                    queries(nxt, 3)
                invert(cur, 3)
                if nxt:
                    maxima(nxt, 2)
                divide(cur, 3)
                if nxt:
                    for pair in range(3, 7):
                        maxima(nxt, pair)
                output(cur, 0)
                if nxt:
                    maxima(nxt, 7)
                    maxima_parts(nxt)
                output(cur, 1)
                output(cur, 2)
                if nxt:
                    maxima_t(nxt)
                output(cur, 3)
                ln2_stats(cur)

            first, final = Blk(0, 0), Blk(BLOCKS // 2 - 1, 1)
            ctx_halves(0)
            ln1_stats(first)
            keys(0)
            values_and_keys_lo(0)
            ctx_halves(1)
            ln1(first)
            keys(1)
            for c in range(DC):
                halves(first, c)
            values_and_keys_lo(1)
            for m in range(DC):
                queries(first, m)
            for pair in range(PAIRS):
                maxima(first, pair)
            maxima_parts(first)
            maxima_t(first)
            step(first, Blk(0, 1), None)
            with dve.Fori(0, BLOCKS // 2 - 1, 1) as j:
                step(Blk(j, 1), Blk(j + 1, 0), Blk(j, 0))
                step(Blk(j + 1, 0), Blk(j + 1, 1), Blk(j, 1))
            step(final, None, Blk(BLOCKS // 2 - 1, 0))
            ln2(final)
            for s in range(SUB):
                routing_lo(final, s)
            for part in range(3):
                route(final, part)
            weights(final)
            targets(final)
            dve.wait_ge(total_full, 1)
            done = [0]

            def link(ins):
                done[0] += 1
                ins.then_inc(made, 1)
                dve.wait_ge(made, done[0])

            by_step = [P, EXPERTS, MOST]
            by_slot = [P, SLOTS, EXPERTS - 1]
            dve.wait_ge(sched_set, SCHED_SET)
            link(dve.tensor_copy(counts[:, :], TOTAL))
            link(dve.tensor_copy(fill_f[:, :], eight_i[:, :]))
            link(dve.tensor_tensor(fill_t[:, :], fill_f[:, :], counts[:, :], ALU.add))
            link(dve.tensor_copy(steps_f[:, :, :], steps_i[:, :, :]))
            link(dve.tensor_copy(slot_f[:, :], slot_i[:, :]))
            link(dve.tensor_tensor(over[:, :, :], counts[:, :].unsqueeze(2).to_broadcast(by_step), steps_f[:, :, :], ALU.is_gt))
            link(dve.tensor_reduce(tiles[:, :], over[:, :, :], AX_X, ALU.add))
            link(dve.tensor_scalar(tiles[:, :], tiles[:, :], 1.0, None, ALU.max))
            link(dve.tensor_tensor_scan(ends[:, :], ones8[:, :], tiles[:, :], 0.0, ALU.mult, ALU.add))
            link(dve.tensor_tensor(passed[:, :, :], slot_f[:, :].unsqueeze(2).to_broadcast(by_slot),
                                   ends[:, 0:EXPERTS - 1].unsqueeze(1).to_broadcast(by_slot), ALU.is_ge))
            link(dve.tensor_reduce(expert_f[:, :], passed[:, :, :], AX_X, ALU.add))
            link(dve.tensor_tensor(passed_n[:, :, :], passed[:, :, :], tiles[:, 0:EXPERTS - 1].unsqueeze(1).to_broadcast(by_slot), ALU.mult))
            link(dve.tensor_reduce(start_f[:, :], passed_n[:, :, :], AX_X, ALU.add))
            link(dve.tensor_tensor(passed_n[:, :, :], passed[:, :, :], sign[:, :].unsqueeze(1).to_broadcast(by_slot), ALU.mult))
            link(dve.tensor_reduce(parity_f[:, :], passed_n[:, :, :], AX_X, ALU.add))
            link(dve.tensor_tensor(off_f[:, :], slot_f[:, :], start_f[:, :], ALU.subtract))
            link(dve.tensor_scalar(row_f[:, :], off_f[:, :], float(P), None, ALU.mult))
            link(dve.scalar_tensor_tensor(out=row_f[:, :], in0=expert_f[:, :], scalar=float(REGION), in1=row_f[:, :], op0=ALU.mult, op1=ALU.add))
            link(dve.tensor_scalar(valid_f[:, :], slot_f[:, :], ends[:, EXPERTS - 1:EXPERTS], None, ALU.is_lt))
            link(dve.scalar_tensor_tensor(out=row_f[:, :], in0=row_f[:, :], scalar=-float(DUMMY), in1=valid_f[:, :], op0=ALU.add, op1=ALU.mult))
            link(dve.tensor_scalar(row_t[:, :], row_f[:, :], float(DUMMY), None, ALU.add))
            link(dve.scalar_tensor_tensor(out=first_f[:, :], in0=off_f[:, :], scalar=0.0, in1=valid_f[:, :], op0=ALU.is_equal, op1=ALU.mult))
            link(dve.scalar_tensor_tensor(out=first_t[:, :], in0=expert_f[:, :], scalar=float(EXPERTS - 1), in1=first_f[:, :], op0=ALU.is_lt, op1=ALU.mult))
            link(dve.tensor_copy(expert_t[:, :], expert_f[:, :]))
            link(dve.tensor_copy(parity_t[:, :], parity_f[:, :]))
            link(dve.tensor_scalar(other_t[:, :], parity_f[:, :], -1.0, 1.0, ALU.mult, ALU.add))
            link(dve.tensor_scalar(stage_t[:, :], expert_f[:, :], 2.0, float(EXPERTS - 1), ALU.add, ALU.min))
            assert done[0] == MADE


def at(i):
    return bass.ds(i, 1)


class Slot:

    def __init__(self, q, r):
        self.q, self.r, self.s = q + r // RING, r % RING, q * RING + r
        self.half = r % 2

    def next(self):
        return Slot(self.q, self.r + 1)


def experts(nc, A, out, rows_sorted, S):
    with ExitStack() as ctx:
        def sb(name, shape, dt):
            return ctx.enter_context(nc.sbuf_tensor(name, shape, dt))

        def bank(name):
            return ctx.enter_context(nc.psum_tensor(name, [P, 512], F32))

        def sem(name):
            return ctx.enter_context(nc.semaphore(name))

        w_raw, w_in = S.w_raw, S.w_in
        w_hi = sb("w_hi", [P, 2, MATS * DC, D], F32R)
        w_lo = sb("w_lo", [P, 2, MATS * DC, D], F32R)
        ident = sb("e_ident", [P, P], F32)
        row_in = [sb(f"row_in{r}", [P, ROW], F32) for r in range(RING)]
        xt_hi, xt_lo = ([sb(f"e_xt_{n}{r}", [P, D], F32R) for r in range(2)] for n in ("hi", "lo"))
        ht_hi, ht_lo = ([sb(f"e_ht_{n}{r}", [P, D], F32R) for r in range(2)] for n in ("hi", "lo"))
        silu = [sb(f"silu{r}", [P, D], F32) for r in range(2)]
        hidden = [sb(f"hidden{r}", [P, D], F32) for r in range(2)]
        y = [sb(f"y{r}", [P, D], F32) for r in range(RING)]
        spare = sb("spare", [1, 2], F32)
        is_first = sb("is_first", [P, RING], F32)
        weight = sb("weight", [P, RING], F32)
        expert_f, row_t, expert_t, first_t, parity_t, other_t, stage_t = (
            S.expert_f, S.row_t, S.expert_t, S.first_t, S.parity_t, S.other_t, S.stage_t)

        psX, psH = bank("psX"), bank("psH")
        psG, psU, psY = ([bank(f"{n}{r}") for r in range(2)] for n in ("psG", "psU", "psY"))

        consts = sem("e_consts")
        w_halves, w_split = sem("w_halves"), sem("w_split")
        rows_landed = [sem(f"rows_landed{r}") for r in range(RING)]
        xt_full, xt_hi_done, xt_done = sem("e_xt_full"), sem("e_xt_hi_done"), sem("e_xt_done")
        gate_full, up_full, silu_done, hidden_done = sem("gate_full"), sem("up_full"), sem("silu_done"), sem("hidden_done")
        ht_full, ht_hi_done, ht_done = sem("ht_full"), sem("ht_hi_done"), sem("ht_done")
        y_full, w_step, y_done, added = sem("y_full"), sem("w_step"), sem("y_done"), sem("added")
        held = sem("held")
        CONSTS = 3
        LOOPED = (SLOTS - 3) // RING
        assert LOOPED * RING == SLOTS - 3
        FINAL = Slot(0, SLOTS - 1)

        block = ctx.enter_context(nc.Block())

        @block.sync
        def _(sp):
            def load(k):
                row = sp.value_load(row_t[0:1, at(k.s)], min_val=0, max_val=DUMMY)
                wait(sp, added, (k.s - RING) * 16 + 16)
                sp.dma_start(row_in[k.r][:, :], rows_sorted[bass.ds(row, P), :]).then_inc(rows_landed[k.r], 16)

            for r in range(RING):
                load(Slot(0, r))
            with sp.Fori(1, SLOTS // RING, 1) as i:
                for r in range(RING):
                    load(Slot(i, r))
            for s in range(SLOTS // RING * RING, SLOTS):
                load(Slot(0, s))

        @block.gpsimd
        def _(pool):
            pool.memset(ident[:, :], 0.0).then_inc(consts, 1)
            pool.memset(spare[:, :], 0.0).then_inc(consts, 1)
            pool.wait_ge(consts, 2)
            pool.affine_select(out=ident[:, :], in_=ident[:, :], compare_op=ALU.not_equal, fill=1.0, base=0,
                               pattern=[[-1, P]], channel_multiplier=1).then_inc(consts, 1)
            pool.wait_ge(w_split, MATS)
            stage(pool, A, S, 1)

            def slot(k):
                pool.wait_ge(y_done, k.s + 1)
                wait(pool, added, k.s * 16)
                hold(pool, spare, held, k.s)
                pool.indirect_dma_start(
                    out=out, out_offset=bass.IndirectOffsetOnAxis(ap=row_in[k.r][:, TOKEN:TOKEN + 1].bitcast(U32), axis=0),
                    in_=y[k.r][:, :], in_offset=None, bounds_check=TOKENS + P - 1, oob_is_err=True,
                    compute_op=ALU.add).then_inc(added, 16)
                first = pool.value_load(first_t[0:1, at(k.s)], min_val=0, max_val=1)
                with pool.If(first > 0):
                    e = pool.value_load(expert_t[0:1, at(k.s)], min_val=0, max_val=EXPERTS - 1)
                    after = pool.value_load(stage_t[0:1, at(k.s)], min_val=0, max_val=EXPERTS - 1)
                    pool.wait_ge(w_split, (e + 2) * MATS)
                    stage(pool, A, S, after)

            slot(Slot(0, 0))
            for u in range(RING):
                slot(Slot(0, 1 + u))
            with pool.Fori(1, LOOPED, 1) as i:
                for u in range(RING):
                    slot(Slot(i, 1 + u))
            for s in range(SLOTS - 2, SLOTS):
                slot(Slot(0, s))
            pool.wait_ge(added, 16 * SLOTS)
            for m in range(MATS):
                pool.wait_ge(w_in[m], 16 * (EXPERTS + 1))

        @block.scalar
        def _(act):
            def xt(k):
                act.wait_ge(xt_full, k.s + 1)
                wait(act, up_full, k.s - 1)
                act.activation(xt_hi[k.half][:, :], psX[:, :], ACT.Copy).then_inc(xt_hi_done, 1)

            def ht(k):
                act.wait_ge(ht_full, k.s + 1)
                wait(act, y_full, k.s - 1)
                act.activation(ht_hi[k.half][:, :], psH[:, :], ACT.Copy).then_inc(ht_hi_done, 1)

            def gate(k):
                act.wait_ge(gate_full, k.s + 1)
                wait(act, hidden_done, k.s - 1)
                act.activation(silu[k.half][:, :], psG[k.half][:, :], ACT.Silu).then_inc(silu_done, 1)

            def result(k):
                act.wait_ge(y_full, k.s + 1)
                act.wait_ge(w_step, k.s * 2 + 2)
                wait(act, added, (k.s - RING) * 16 + 16)
                act.activation(y[k.r][:, :], psY[k.half][:, :], ACT.Copy, scale=weight[:, k.r:k.r + 1]).then_inc(y_done, 1)

            def weights_hi(parity, n, m):
                act.wait_ge(w_in[m], 16 * (n + 1))
                ms = slice(m * DC, m * DC + DC)
                act.activation(w_hi[:, at(parity), ms, :].rearrange("p a c n -> p (a c n)"),
                               w_raw[:, ms, :].rearrange("p c n -> p (c n)"), ACT.Copy).then_inc(w_halves, 1)

            def next_weights(k, ms):
                with act.If(act.value_load(first_t[0:1, at(k.s)], min_val=0, max_val=1) > 0):
                    e = act.value_load(expert_t[0:1, at(k.s)], min_val=0, max_val=EXPERTS - 1)
                    other = act.value_load(other_t[0:1, at(k.s)], min_val=0, max_val=1)
                    for m in ms:
                        weights_hi(other, e + 1, m)

            def body(k):
                xt(k.next())
                ht(k.prev)
                next_weights(k.prev, (0, 1))
                gate(k)
                next_weights(k.prev, (2,))
                result(k.prev)

            weights_hi(0, 0, 0)
            weights_hi(0, 0, 1)
            xt(Slot(0, 0))
            xt(Slot(0, 1))
            weights_hi(0, 0, 2)
            gate(Slot(0, 0))
            for u in range(RING):
                body(with_prev(0, 1 + u))
            with act.Fori(1, LOOPED, 1) as i:
                for u in range(RING):
                    body(with_prev(i, 1 + u))
            body(with_prev(0, SLOTS - 2))
            ht(Slot(0, SLOTS - 2))
            next_weights(Slot(0, SLOTS - 2), (0, 1))
            gate(FINAL)
            next_weights(Slot(0, SLOTS - 2), (2,))
            result(Slot(0, SLOTS - 2))
            ht(FINAL)
            result(FINAL)

        @block.tensor
        def _(pe):
            def split3(dst, hi, lo, par, m):
                for c in range(DC):
                    wh = w_hi[:, at(par), m * DC + c, :].rearrange("p a n -> p (a n)")
                    wl = w_lo[:, at(par), m * DC + c, :].rearrange("p a n -> p (a n)")
                    cs = slice(c * P, c * P + P)
                    pe.matmul(dst[:, :], hi[:, cs], wh, start=c == 0, stop=False)
                    pe.matmul(dst[:, :], hi[:, cs], wl, start=False, stop=False)
                    last = pe.matmul(dst[:, :], lo[:, cs], wh, start=False, stop=c == DC - 1)
                return last

            def xt(k):
                pe.wait_ge(rows_landed[k.r], k.q * 16 + 16)
                wait(pe, xt_done, k.s)
                for c in range(DC):
                    last = pe.transpose(psX[:, c * P:c * P + P], row_in[k.r][:, c * P:c * P + P], ident[:, :])
                last.then_inc(xt_full, 1)

            def ht(k):
                pe.wait_ge(hidden_done, k.s + 1)
                wait(pe, ht_done, k.s)
                for c in range(DC):
                    last = pe.transpose(psH[:, c * P:c * P + P], hidden[k.half][:, c * P:c * P + P], ident[:, :])
                last.then_inc(ht_full, 1)

            def weights_of(k):
                return (pe.value_load(expert_t[0:1, at(k.s)], min_val=0, max_val=EXPERTS - 1),
                        pe.value_load(parity_t[0:1, at(k.s)], min_val=0, max_val=1))

            def gate_up(k, e, par):
                pe.wait_ge(w_split, e * MATS + 1)
                pe.wait_ge(xt_done, k.s + 1)
                wait(pe, hidden_done, k.s - 1)
                split3(psG[k.half], xt_hi[k.half], xt_lo[k.half], par, 0).then_inc(gate_full, 1)
                pe.wait_ge(w_split, e * MATS + 2)
                split3(psU[k.half], xt_hi[k.half], xt_lo[k.half], par, 1).then_inc(up_full, 1)

            def down(k, e, par):
                pe.wait_ge(w_split, e * MATS + MATS)
                pe.wait_ge(ht_done, k.s + 1)
                wait(pe, y_done, k.s - 1)
                split3(psY[k.half], ht_hi[k.half], ht_lo[k.half], par, 2).then_inc(y_full, 1)

            def body(k):
                now = weights_of(k)
                xt(k.next())
                ht(k.prev)
                gate_up(k, *now)
                down(k.prev, *weights_of(k.prev))

            pe.wait_ge(consts, CONSTS)
            xt(Slot(0, 0))
            xt(Slot(0, 1))
            gate_up(Slot(0, 0), *weights_of(Slot(0, 0)))
            for u in range(RING):
                body(with_prev(0, 1 + u))
            with pe.Fori(1, LOOPED, 1) as i:
                for u in range(RING):
                    body(with_prev(i, 1 + u))
            body(with_prev(0, SLOTS - 2))
            ht(Slot(0, SLOTS - 2))
            gate_up(FINAL, *weights_of(FINAL))
            down(Slot(0, SLOTS - 2), *weights_of(Slot(0, SLOTS - 2)))
            ht(FINAL)
            down(FINAL, *weights_of(FINAL))

        @block.vector
        def _(dve):
            def xt(k):
                dve.wait_ge(xt_hi_done, k.s + 1)
                dve.tensor_tensor(xt_lo[k.half][:, :], psX[:, :], xt_hi[k.half][:, :].bitcast(F32), ALU.subtract).then_inc(xt_done, 1)

            def ht(k):
                dve.wait_ge(ht_hi_done, k.s + 1)
                dve.tensor_tensor(ht_lo[k.half][:, :], psH[:, :], ht_hi[k.half][:, :].bitcast(F32), ALU.subtract).then_inc(ht_done, 1)

            def combine(k):
                dve.wait_ge(rows_landed[k.r], k.q * 16 + 16)
                wait(dve, y_done, k.s - RING + 1)
                dve.tensor_tensor(is_first[:, k.r:k.r + 1], row_in[k.r][:, FIRST_EXPERT:FIRST_EXPERT + 1],
                                  expert_f[:, at(k.s)], ALU.is_equal).then_inc(w_step, 1)
                dve.wait_ge(w_step, k.s * 2 + 1)
                dve.scalar_tensor_tensor(out=weight[:, k.r:k.r + 1], in0=is_first[:, k.r:k.r + 1],
                                         scalar=row_in[k.r][:, W_DIFF:W_DIFF + 1], in1=row_in[k.r][:, W_LOW:W_LOW + 1],
                                         op0=ALU.mult, op1=ALU.add).then_inc(w_step, 1)

            def hide(k):
                dve.wait_ge(silu_done, k.s + 1)
                dve.wait_ge(up_full, k.s + 1)
                wait(dve, ht_full, k.s - 1)
                dve.tensor_tensor(hidden[k.half][:, :], psU[k.half][:, :], silu[k.half][:, :], ALU.mult).then_inc(hidden_done, 1)

            def weights_lo(parity, n, m):
                dve.wait_ge(w_halves, n * MATS + m + 1)
                ms = slice(m * DC, m * DC + DC)
                dve.tensor_tensor(w_lo[:, at(parity), ms, :].rearrange("p a c n -> p (a c n)"),
                                  w_raw[:, ms, :].rearrange("p c n -> p (c n)"),
                                  w_hi[:, at(parity), ms, :].rearrange("p a c n -> p (a c n)").bitcast(F32),
                                  ALU.subtract).then_inc(w_split, 1)

            def next_weights(k, ms):
                with dve.If(dve.value_load(first_t[0:1, at(k.s)], min_val=0, max_val=1) > 0):
                    e = dve.value_load(expert_t[0:1, at(k.s)], min_val=0, max_val=EXPERTS - 1)
                    other = dve.value_load(other_t[0:1, at(k.s)], min_val=0, max_val=1)
                    for m in ms:
                        weights_lo(other, e + 1, m)

            def body(k):
                xt(k.next())
                combine(k)
                ht(k.prev)
                next_weights(k.prev, (0, 1))
                hide(k)
                next_weights(k.prev, (2,))

            weights_lo(0, 0, 0)
            xt(Slot(0, 0))
            weights_lo(0, 0, 1)
            xt(Slot(0, 1))
            weights_lo(0, 0, 2)
            combine(Slot(0, 0))
            hide(Slot(0, 0))
            for u in range(RING):
                body(with_prev(0, 1 + u))
            with dve.Fori(1, LOOPED, 1) as i:
                for u in range(RING):
                    body(with_prev(i, 1 + u))
            body(with_prev(0, SLOTS - 2))
            combine(FINAL)
            ht(Slot(0, SLOTS - 2))
            next_weights(Slot(0, SLOTS - 2), (0, 1))
            hide(FINAL)
            next_weights(Slot(0, SLOTS - 2), (2,))
            ht(FINAL)


def with_prev(q, r):
    k = Slot(q, r)
    k.prev = Slot(q, r - 1)
    return k


def build(nc, A, out):
    rows_sorted = nc.dram_tensor("rows_sorted", [SORTED_ROWS, ROW], F32).ap()
    with ExitStack() as ctx:
        shared = Shared(nc, ctx)
        attention_and_routing(nc, A, out, rows_sorted, shared)
        experts(nc, A, out, rows_sorted, shared)


_INS = {"x": "x", "ctx": "ctx_1024", "g_xattn": "g_xattn", "g_ffn": "g_ffn", "Wq": "L0_xattn_Wq", "bq": "L0_xattn_bq",
        "Wo": "L0_xattn_Wo", "bo": "L0_xattn_bo", "router_w": "L0_ffn_router_w", "router_b": "L0_ffn_router_b",
        "we_gate": "L0_ffn_we_gate", "we_up": "L0_ffn_we_up", "we_down": "L0_ffn_we_down"}


def kernel(**inputs):
    import concourse.bacc as bacc
    from concourse.bass_utils import run_bass_kernel_spmd

    nc = bacc.Bacc("TRN2", target_bir_lowering=False, num_devices=1)
    arrays, args = {}, {}
    for short, name in _INS.items():
        a = np.ascontiguousarray(inputs[name])
        arrays[f"in_{short}"] = a
        args[short] = nc.dram_tensor(f"in_{short}", a.shape, mybir.dt.from_np(a.dtype), kind="ExternalInput").ap()
    out = nc.dram_tensor("out_rows", [TOKENS + P, D], F32, kind="ExternalOutput").ap()
    build(nc, args, out)
    r = run_bass_kernel_spmd(nc, [arrays], core_ids=[0])
    return r.results[0]["out_rows"][:TOKENS].reshape(BATCHES, SEQ, D)
```
